# Optimizing a Trainium2 kernel written in Bass

```python
import numpy as np
import jax
import jax.numpy as jnp

def _softmax(x, axis=-1):
    return jax.nn.softmax(x, axis=axis)

def _gelu(x):
    return jax.nn.gelu(x, approximate=True)

def _silu(x):
    return jax.nn.silu(x)

def _sigmoid(x):
    return jax.nn.sigmoid(x)

def _layernorm(x, axis=-1, eps=1e-05):
    m = jnp.mean(x, axis=axis, keepdims=True)
    v = jnp.var(x, axis=axis, keepdims=True)
    return (x - m) / jnp.sqrt(v + eps)

def _scatter_add(tgt, idx, src, axis=0):
    return tgt.at[idx].add(src)

def _segment_sum(src, seg, n):
    return jax.ops.segment_sum(src, seg, n)
kernel_name = 'mk_gnn_preln_d1_gnn_r16_510f3c'

def setup_inputs(seed: int=0):
    np.random.seed(seed)
    _w = jnp.asarray

    def _rec_inputs():
        import jax
        import jax.numpy as jnp
        _gk = jax.random.key(seed)
        x = -0.000202 + 1 * jax.random.normal(jax.random.fold_in(_gk, 1), (6250, 128), jnp.float32)
        _s = jax.random.randint(jax.random.fold_in(_gk, 2), (100000,), 0, 6250, jnp.int32)
        _d = jax.random.randint(jax.random.fold_in(_gk, 3), (100000,), 0, 6250, jnp.int32)
        _loop = jnp.arange(6250, dtype=jnp.int32)
        src = jnp.concatenate([_s, _d, _loop])
        dst = jnp.concatenate([_d, _s, _loop])
        _o = jnp.argsort(dst, stable=True)
        src = src[_o]
        dst = dst[_o]
        return (x, src, dst)
    x, src, dst = _rec_inputs()

    def _L0_gnn_setup():
        import jax, jax.numpy as jnp
        import numpy as np
        N = 3125
        E = 50000
        IN_C, HID_C, OUT_C = (128, 256, 128)
        EPS = 1e-05

        def _lin_params(key, out_f, in_f, bias=True):
            kw, kb = jax.random.split(key)
            bound = 1.0 / np.sqrt(in_f)
            W = jax.random.uniform(kw, (out_f, in_f), jnp.float32, -bound, bound)
            if bias:
                b = jax.random.uniform(kb, (out_f,), jnp.float32, -bound, bound)
                return (W, b)
            return (W, None)

        def _mean_agg(x, src, dst, n):
            msg_sum = jax.ops.segment_sum(x[src], dst, num_segments=n)
            cnt = jax.ops.segment_sum(jnp.ones((src.shape[0], 1), x.dtype), dst, num_segments=n)
            return msg_sum / jnp.maximum(cnt, 1.0)

        def _sage_conv(x, src, dst, Wl, bl, Wr):
            agg = _mean_agg(x, src, dst, x.shape[0])
            out = agg @ Wl.T + bl + x @ Wr.T
            return out

        def _batch_norm(x, gamma, beta):
            mu = jnp.mean(x, axis=0)
            var = jnp.mean(jnp.square(x - mu), axis=0)
            return (x - mu) * jax.lax.rsqrt(var + EPS) * gamma + beta
        key = jax.random.key(seed)
        ks = jax.random.split(key, 12)
        x = jax.random.normal(ks[0], (N, IN_C), jnp.float32)
        edge_index = jax.random.randint(ks[1], (2, E), 0, N, dtype=jnp.int64)
        Wl0, bl0 = _lin_params(ks[2], HID_C, IN_C)
        Wr0, _ = _lin_params(ks[3], HID_C, IN_C, bias=False)
        Wl1, bl1 = _lin_params(ks[4], HID_C, HID_C)
        Wr1, _ = _lin_params(ks[5], HID_C, HID_C, bias=False)
        Wl2, bl2 = _lin_params(ks[6], OUT_C, HID_C)
        Wr2, _ = _lin_params(ks[7], OUT_C, HID_C, bias=False)
        gamma0 = jnp.ones((HID_C,), jnp.float32)
        beta0 = jnp.zeros((HID_C,), jnp.float32)
        gamma1 = jnp.ones((HID_C,), jnp.float32)
        beta1 = jnp.zeros((HID_C,), jnp.float32)
        return {'x': x, 'edge_index': edge_index, 'Wl0': Wl0, 'bl0': bl0, 'Wr0': Wr0, 'gamma0': gamma0, 'beta0': beta0, 'Wl1': Wl1, 'bl1': bl1, 'Wr1': Wr1, 'gamma1': gamma1, 'beta1': beta1, 'Wl2': Wl2, 'bl2': bl2, 'Wr2': Wr2}
    _L0_gnn_all = _L0_gnn_setup()
    _L0_gnn_in = {k: v for k, v in _L0_gnn_all.items() if k in ('Wl0', 'bl0', 'Wr0', 'gamma0', 'beta0', 'Wl1', 'bl1', 'Wr1', 'gamma1', 'beta1', 'Wl2', 'bl2', 'Wr2')}
    del _L0_gnn_all
    return {'x': x, 'src': src, 'dst': dst, 'L0_gnn_Wl0': _L0_gnn_in['Wl0'], 'L0_gnn_bl0': _L0_gnn_in['bl0'], 'L0_gnn_Wr0': _L0_gnn_in['Wr0'], 'L0_gnn_gamma0': _L0_gnn_in['gamma0'], 'L0_gnn_beta0': _L0_gnn_in['beta0'], 'L0_gnn_Wl1': _L0_gnn_in['Wl1'], 'L0_gnn_bl1': _L0_gnn_in['bl1'], 'L0_gnn_Wr1': _L0_gnn_in['Wr1'], 'L0_gnn_gamma1': _L0_gnn_in['gamma1'], 'L0_gnn_beta1': _L0_gnn_in['beta1'], 'L0_gnn_Wl2': _L0_gnn_in['Wl2'], 'L0_gnn_bl2': _L0_gnn_in['bl2'], 'L0_gnn_Wr2': _L0_gnn_in['Wr2']}

def reference(x, src, dst, L0_gnn_Wl0, L0_gnn_bl0, L0_gnn_Wr0, L0_gnn_gamma0, L0_gnn_beta0, L0_gnn_Wl1, L0_gnn_bl1, L0_gnn_Wr1, L0_gnn_gamma1, L0_gnn_beta1, L0_gnn_Wl2, L0_gnn_bl2, L0_gnn_Wr2):
    import jax
    import jax.numpy as jnp

    def _L0_gnn_ref(x, edge_index, Wl0, bl0, Wr0, gamma0, beta0, Wl1, bl1, Wr1, gamma1, beta1, Wl2, bl2, Wr2):
        import jax, jax.numpy as jnp
        import numpy as np
        N = 3125
        E = 50000
        IN_C, HID_C, OUT_C = (128, 256, 128)
        EPS = 1e-05

        def _lin_params(key, out_f, in_f, bias=True):
            kw, kb = jax.random.split(key)
            bound = 1.0 / np.sqrt(in_f)
            W = jax.random.uniform(kw, (out_f, in_f), jnp.float32, -bound, bound)
            if bias:
                b = jax.random.uniform(kb, (out_f,), jnp.float32, -bound, bound)
                return (W, b)
            return (W, None)

        def _mean_agg(x, src, dst, n):
            msg_sum = jax.ops.segment_sum(x[src], dst, num_segments=n)
            cnt = jax.ops.segment_sum(jnp.ones((src.shape[0], 1), x.dtype), dst, num_segments=n)
            return msg_sum / jnp.maximum(cnt, 1.0)

        def _sage_conv(x, src, dst, Wl, bl, Wr):
            agg = _mean_agg(x, src, dst, x.shape[0])
            out = agg @ Wl.T + bl + x @ Wr.T
            return out

        def _batch_norm(x, gamma, beta):
            mu = jnp.mean(x, axis=0)
            var = jnp.mean(jnp.square(x - mu), axis=0)
            return (x - mu) * jax.lax.rsqrt(var + EPS) * gamma + beta
        src, dst = (edge_index[0], edge_index[1])
        h = _sage_conv(x, src, dst, Wl0, bl0, Wr0)
        h = jax.nn.relu(_batch_norm(h, gamma0, beta0))
        h = _sage_conv(h, src, dst, Wl1, bl1, Wr1)
        h = jax.nn.relu(_batch_norm(h, gamma1, beta1))
        h = _sage_conv(h, src, dst, Wl2, bl2, Wr2)
        return jax.nn.log_softmax(h, axis=-1)
    edge_index = jnp.stack([src, dst])
    h = jnp.maximum(_layernorm(x, axis=-1), 0.0)
    x = x + _L0_gnn_ref(h, edge_index, L0_gnn_Wl0, L0_gnn_bl0, L0_gnn_Wr0, L0_gnn_gamma0, L0_gnn_beta0, L0_gnn_Wl1, L0_gnn_bl1, L0_gnn_Wr1, L0_gnn_gamma1, L0_gnn_beta1, L0_gnn_Wl2, L0_gnn_bl2, L0_gnn_Wr2)
    return x

_drawn_inputs = setup_inputs


def setup_inputs(seed=0):
    import zlib

    import numpy as np

    out = dict(_drawn_inputs(seed))
    spreads = {'L0_gnn_gamma0': (1.0, 0.6),
     'L0_gnn_beta0': (0.0, 0.8),
     'L0_gnn_gamma1': (1.0, 0.6),
     'L0_gnn_beta1': (0.0, 0.8)}
    factors = {'L0_gnn_Wl0': 3.239,
     'L0_gnn_bl0': 8.0,
     'L0_gnn_Wl1': 3.851,
     'L0_gnn_bl1': 8.0,
     'L0_gnn_bl2': 8.0}
    for name, (base, spread) in spreads.items():
        noise = np.random.default_rng([zlib.crc32(name.encode()), seed]).standard_normal(out[name].shape)
        drawn = base * np.exp(spread * noise) if base else spread * noise
        out[name] = jnp.asarray(drawn.astype(out[name].dtype))
    for name, factor in factors.items():
        out[name] = (out[name] * factor).astype(out[name].dtype)
    return out
```

```python
from contextlib import ExitStack

import concourse.bass as bass
from concourse import mybir
from concourse.alu_op_type import AluOpType as ALU

F32 = mybir.dt.float32
F16 = mybir.dt.float16
I32 = mybir.dt.int32
U32 = mybir.dt.uint32
ACT = mybir.ActivationFunctionType
AX = mybir.AxisListType

P = 128
GD = 5
WIN = 256
BD = 250
GPB = BD // GD
PPB = GPB // 2
PW = 248
EPS = 1e-5
S0 = 1024.0
NPB = 12


class Stream:

    def __init__(self, eng, sem):
        self.eng, self.sem, self.n, self.seen = eng, sem, 0, {}

    def mark(self, ins):
        ins.then_inc(self.sem, 1)
        self.n += 1
        return (self.sem, self.n)

    def last(self):
        return (self.sem, self.n)

    def need(self, *tokens):
        for t in tokens:
            if t is None:
                continue
            sem, val = t
            if self.seen.get(sem.name, 0) < val:
                self.eng.wait_ge(sem, val)
                self.seen[sem.name] = val

    def state(self):
        return self.n, dict(self.seen)

    def restore(self, s):
        self.n, self.seen = s[0], dict(s[1])


class Slot:

    def __init__(self, sem):
        self.sem, self.n = sem, 0

    def mark(self, ins):
        ins.then_inc(self.sem, 16)
        self.n += 16
        return (self.sem, self.n)


def gnn_program(nc, n_edges, x, pairs, dst_rows, samples, const_f, iota_h, WlT, WrT, vecs, out):
    N, F0 = x.shape
    E = n_edges
    EP = pairs.shape[0] * pairs.shape[1]
    R = dst_rows.shape[0]
    NA = -(-N // P)
    LAST = N - P * (NA - 1)
    NG = N // GD
    NJ = -(-NG // P)
    NB = N // BD
    NT = -(-E // P)
    NW = GD * NA
    assert N % BD == 0 and NW <= PW and 2 * NW <= 512 and NT * P <= EP

    flat_pairs = pairs.rearrange("r c two -> (r c) two")

    with ExitStack() as ctx:
        def sb(name, shape, dt=F32):
            return ctx.enter_context(nc.sbuf_tensor(name, shape, dt))

        def sem(name):
            return ctx.enter_context(nc.semaphore(name))

        C_dram = nc.dram_tensor("c_blocks", [NB, P, NA * BD], F16).ap()
        rc_dram = nc.dram_tensor("rc_row", [NJ * P * GD], F32).ap()
        tab_dram = nc.dram_tensor("part_rows", [NA * P, 512], F16).ap()

        bank = [ctx.enter_context(nc.psum_tensor(f"bank{i}", [P, 512], F32)) for i in range(8)]

        Z = sb("Z", [P, 2, NA * P])
        parts = sb("parts", [P, NA * 512], F16)
        ring = sb("ring", [P, 3, NA * BD], F16)
        onehot_d = sb("onehot_d", [P, NPB, PW], F16)
        onehot_s = sb("onehot_s", [P, NPB, P], F16)
        agm = sb("agm", [P, 2, 2, BD])
        rcb = sb("rcb", [P, 2, BD])
        iota = sb("iota", [P, 256], F16)
        cf = sb("cf", [P, NJ + P])
        thr = cf[:, 0:NJ]
        ident = cf[:, NJ:NJ + P]
        wl = [sb("wl0", [P, 1, 256]), sb("wl1", [P, 2, 256]), sb("wl2", [P, 2, 128])]
        wr = [sb("wr0", [P, 1, 256]), sb("wr1", [P, 2, 256]), sb("wr2", [P, 2, 128])]
        vec = sb("vec", [P, 13])
        bias = [vec[:, 0:2], vec[:, 2:4], vec[:, 4:5]]
        gamma = [vec[:, 5:7], vec[:, 7:9]]
        beta = [vec[:, 9:11], vec[:, 11:13]]
        ones = sb("ones", [P, P])
        ones_h = sb("ones_h", [P, P], F16)
        zeros_h = sb("zeros_h", [P, BD], F16)
        c1 = sb("c1", [P, NJ])
        c2 = sb("c2", [P, NJ])
        row = sb("row", [P, NJ])
        row_i = sb("row_i", [P, NJ], U32)
        first = sb("first", [P, NJ])
        first_i = sb("first_i", [P, NJ], U32)
        sgn = sb("sgn", [P, NJ, 6])
        cut = sb("cut", [P, 6])
        epsc = sb("epsc", [P, 1])
        cntg = sb("cntg", [P, NJ, GD])
        tot = sb("tot", [P, 4])
        flag = sb("flag", [P, 1], I32)
        st = sb("st", [P, 2, max(NB, 25), 6])
        mv = sb("mv", [P, 2, 2])
        bnw = sb("bnw", [P, 12, 2])
        bnwi = sb("bnwi", [P, 2, 2], I32)
        mvx = sb("mvx", [P, NA, 2])
        rsx = sb("rsx", [P, 4, NA])
        isp = sb("isp", [P, 1])
        sm = sb("sm", [P, 4, NA])
        ex = sb("ex", [P, 2, P])
        dd = sb("dd", [P, 4, 2, P])
        spr = sb("spr", [P, 3, P])
        spi = sb("spi", [P, 2, P], I32)
        slow_f = sb("slow_f", [P, 2])
        slow_i = sb("slow_i", [P, 1], U32)

        small = parts[:, 0:NA * 256].rearrange("p (a s f) -> p a s f", a=NA, s=2)
        wide = parts[:, :].rearrange("p (a s f) -> p a s f", a=NA, s=2)
        upper = parts[:, NA * 256:NA * 512].bitcast(F32)
        tab = upper[:, 0:NJ * 512].rearrange("p (j v h g) -> p j v h g", j=NJ, v=2, h=2) \
            if NJ * 512 <= NA * 128 else sb("tab", [P, NJ, 2, 2, P])
        xres = upper.rearrange("p (a f) -> p a f", a=NA)
        X = Z[:, 1, :].rearrange("p (a f) -> p a f", a=NA)
        rf = ring[:, :, :].rearrange("p s n -> p (s n)").bitcast(F32)
        need_ring = 2 * R + NJ * 256 * 2 + NJ * 512 * 2 + 512 + max(R, 256)
        if need_ring > 3 * NA * BD // 2:
            rf = sb("scratch", [P, need_ring])[:, :]
        at = [0]

        def scratch(n):
            at[0] += n
            return rf[:, at[0] - n:at[0]]

        smp_i = scratch(R).bitcast(I32)
        smp = scratch(R)
        rows_i = scratch(NJ * 256).bitcast(I32).rearrange("p (j n) -> p j n", j=NJ)
        rows_f = scratch(NJ * 256).rearrange("p (j n) -> p j n", j=NJ)
        win = scratch(NJ * 512).bitcast(I32).rearrange("p (j n two) -> p j n two", j=NJ, two=2)
        vb = scratch(NJ * 512).rearrange("p (j v n) -> p j v n", j=NJ, v=2)
        vd = scratch(256)
        asrc = scratch(256).bitcast(I32)
        junk = scratch(max(R, 256))
        blk = [ring[:, s, :].rearrange("p (a d) -> p a d", a=NA) for s in range(3)]
        ed = ring[:, :, :].rearrange("p s n -> p (s n)").bitcast(I32)[:, 0:NT * 2] \
            .rearrange("p (t two) -> p t two", two=2)

        pe = Stream(nc.tensor, sem("s_pe"))
        dve = Stream(nc.vector, sem("s_dve"))
        act = Stream(nc.scalar, sem("s_act"))
        pool = Stream(nc.gpsimd, sem("s_pool"))
        sp = Stream(nc.sync, sem("s_sp"))
        streams = [pe, dve, act, pool, sp]
        q_c = Slot(sem("q_c"))
        q_x = Slot(sem("q_x"))
        q_w = Slot(sem("q_w"))
        q_row = [Slot(sem(f"q_row{j}")) for j in range(NJ)]
        q_win = [Slot(sem(f"q_win{j}")) for j in range(NJ)]
        q_rc = Slot(sem("q_rc"))
        q_blk = [Slot(sem(f"q_blk{i}")) for i in range(3)]
        q_st = [Slot(sem(f"q_st{i}")) for i in range(3)]
        q_rcb = [Slot(sem(f"q_rcb{i}")) for i in range(2)]
        q_xr = Slot(sem("q_xr"))
        q_o = [Slot(sem(f"q_o{i}")) for i in range(4)]
        q_tab = Slot(sem("q_tab"))
        s_g = sem("s_gather")
        s_it = {k: sem(f"s_it_{k}") for k in ("idx", "hot", "pe", "col", "go")}
        slots = [q_c, q_x, q_w, q_rc, q_xr, q_tab] + q_row + q_win + q_blk + q_st + q_rcb + q_o

        def seq(s, ins):
            t = s.mark(ins)
            s.need(t)
            return t

        q_c.mark(sp.eng.dma_start(cf[:, :], const_f))
        q_c.mark(sp.eng.dma_start(smp_i, samples.to_broadcast((P, R))))
        t_c = q_c.mark(sp.eng.dma_start(iota[:, :], iota_h))
        for a0, a1, rows in ((0, NA - 1, P), (NA - 1, NA, LAST)):
            t_x = q_x.mark(sp.eng.dma_start(
                X[0:rows, a0:a1, :], x[a0 * P:a0 * P + (a1 - a0) * rows, :].rearrange("(a p) f -> p a f", p=rows)))
        for layer in range(3):
            for w, src in ((wl[layer], WlT[layer]), (wr[layer], WrT[layer])):
                q_w.mark(sp.eng.dma_start(w[:, :, :], src.rearrange("(k p) m -> p k m", p=P)))
        t_w = q_w.mark(sp.eng.dma_start(vec[:, :], vecs))

        pool.mark(nc.gpsimd.memset(ones[:, :], 1.0))
        pool.mark(nc.gpsimd.memset(ones_h[:, :], 1.0))
        pool.mark(nc.gpsimd.memset(epsc[:, :], EPS))
        for k in range(6):
            pool.mark(nc.gpsimd.memset(cut[:, k:k + 1], 0.5 - NA * k))
        t_set = pool.mark(nc.gpsimd.memset(zeros_h[:, :], 0.0))

        dve.need(t_c)
        seq(dve, nc.vector.tensor_copy(smp, smp_i))
        for j in range(NJ):
            dve.mark(nc.vector.tensor_scalar(junk[:, 0:R], smp, thr[:, j:j + 1], None, ALU.is_lt, ALU.add,
                                             accum_out=c1[:, j:j + 1]))
            dve.need(dve.last())
        seq(dve, nc.vector.tensor_scalar(row[:, :], c1[:, :], -1.0, 0.0, ALU.add, ALU.max))
        t_row = seq(dve, nc.vector.tensor_copy(row_i[:, :], row[:, :]))
        pool.need(t_row)
        t_rows = [q_row[j].mark(nc.gpsimd.indirect_dma_start(
            out=rows_i[:, j, :], out_offset=None, in_=dst_rows,
            in_offset=bass.IndirectOffsetOnAxis(ap=row_i[:, j:j + 1], axis=0))) for j in range(NJ)]

        dve.need(t_x)
        xst = st[:, 0, :, :].rearrange("p n s -> p (n s)")
        for a in range(NA):
            r = P if a < NA - 1 else LAST
            s = xst[0:r, 6 * (a % 25):6 * (a % 25) + 6]
            dve.need(dve.mark(nc.vector.bn_stats(s, X[0:r, a, :])))
            dve.mark(nc.vector.bn_aggr(mvx[0:r, a, :], s))
        t_mvx = dve.last()
        for j in range(NJ):
            dve.need(t_rows[j])
            seq(dve, nc.vector.tensor_copy(rows_f[:, j, :], rows_i[:, j, :]))
            seq(dve, nc.vector.tensor_scalar(junk[:, 0:256], rows_f[:, j, :], thr[:, j:j + 1], None,
                                             ALU.is_lt, ALU.add, accum_out=c2[:, j:j + 1]))
            seq(dve, nc.vector.scalar_tensor_tensor(first[:, j:j + 1], row[:, j:j + 1], 256.0, c2[:, j:j + 1],
                                                    ALU.mult, ALU.add))
            t = seq(dve, nc.vector.tensor_copy(first_i[:, j:j + 1], first[:, j:j + 1]))
            pool.need(t)
            q_win[j].mark(nc.gpsimd.indirect_dma_start(
                out=win[:, j, :, :].rearrange("p n two -> p (n two)"), out_offset=None, in_=flat_pairs,
                in_offset=bass.IndirectOffsetOnAxis(ap=first_i[:, j:j + 1], axis=0)))

        act.need(t_mvx, t_set)
        nfull = NA - 1
        groups = [(slice(0, P), slice(0, nfull)), (slice(0, LAST), slice(nfull, NA))]
        for pr, ar in groups:
            t = act.mark(nc.scalar.activation(rsx[pr, 0, ar], mvx[pr, ar, 1], ACT.Sqrt, bias=epsc[pr, 0:1]))
        dve.need(t)
        for pr, ar in groups:
            seq(dve, nc.vector.reciprocal(rsx[pr, 1, ar], rsx[pr, 0, ar]))
            seq(dve, nc.vector.tensor_scalar(rsx[pr, 2, ar], rsx[pr, 1, ar], S0, None, ALU.mult))
            t = seq(dve, nc.vector.scalar_tensor_tensor(rsx[pr, 3, ar], mvx[pr, ar, 0], -1.0, rsx[pr, 2, ar],
                                                        ALU.mult, ALU.mult))
        act.need(t)
        t_h = []
        for a in range(NA):
            r = P if a < NA - 1 else LAST
            t = act.mark(nc.scalar.activation(X[0:r, a, :], X[0:r, a, :], ACT.Relu,
                                              bias=rsx[0:r, 3, a:a + 1], scale=rsx[0:r, 2, a:a + 1]))
            act.need(t)
            t_h.append(t)
            t = act.mark(nc.scalar.copy(small[0:r, a, 0, :], X[0:r, a, :]))
            dve.need(t)
            dve.mark(nc.vector.tensor_tensor(small[0:r, a, 1, :], X[0:r, a, :], small[0:r, a, 0, :], ALU.subtract))
        t_lo0 = dve.last()

        free = {i: [] for i in range(8)}
        for j in range(NJ):
            dve.need((q_win[j].sem, 16))
            w_src, w_dst = win[:, j, :, 0], win[:, j, :, 1]
            if j:
                dve.need(t_asrc)
            seq(dve, nc.vector.tensor_scalar(asrc, w_src, 7, None, ALU.logical_shift_right))
            act_done = t_sgn if j else None
            dve.need(act_done)
            t_vd = seq(dve, nc.vector.tensor_scalar(vd, w_dst, thr[:, j:j + 1], float(NA), ALU.subtract, ALU.mult))
            dve.mark(nc.vector.tensor_tensor(vb[:, j, 0, :], vd, asrc, ALU.add))
            t_vb = dve.mark(nc.vector.scalar_tensor_tensor(vb[:, j, 1, :], asrc, -128.0, w_src, ALU.mult, ALU.add))
            t_asrc = t_vb
            act.need(t_vd)
            for k in range(6):
                t_sgn = act.mark(nc.scalar.activation(ex[:, :, :].rearrange("p a f -> p (a f)"), vd, ACT.Sign,
                                                      bias=cut[:, k:k + 1], accum_out=sgn[:, j, k:k + 1]))
                act.need(t_sgn)
            b = bank[j % 2]
            pe.need(t_vb, t_c, *free[j % 2])
            for v in range(2):
                for h in range(2):
                    t = pe.mark(nc.tensor.transpose(b[:, 128 * (2 * v + h):128 * (2 * v + h) + 128],
                                                    vb[:, j, v, 128 * h:128 * h + 128], ident))
            act.need(t)
            t = act.mark(nc.scalar.copy(tab[:, j, :, :, :].rearrange("p v h g -> p (v h g)"), b[:, :]))
            free[j % 2] = [t]
        t_tab = t
        dve.need(t_sgn)
        seq(dve, nc.vector.tensor_tensor(cntg[:, :, :], sgn[:, :, 0:GD], sgn[:, :, 1:GD + 1], ALU.subtract))
        seq(dve, nc.vector.tensor_reduce(tot[:, 0:1], cntg[:, :, :], AX.XY, ALU.add))
        pe.need(dve.last(), t_set, *free[0])
        t = pe.mark(nc.tensor.matmul(bank[0][:, 0:1], ones[:, :], tot[:, 0:1], start=True, stop=True))
        seq(dve, nc.vector.tensor_scalar(cntg[:, :, :], cntg[:, :, :], 0.5, 1.0, ALU.mult, ALU.max))
        seq(dve, nc.vector.reciprocal(cntg[:, :, :], cntg[:, :, :]))
        dve.need(t)
        seq(dve, nc.vector.tensor_scalar(tot[:, 1:2], bank[0][:, 0:1], 2.0 * E, None, ALU.is_equal))
        t_flag = seq(dve, nc.vector.tensor_copy(flag[:, :], tot[:, 1:2]))
        free[0] = [t_flag]
        b0 = 1
        for a0 in range(0, NA, 4):
            n = min(4, NA - a0)
            b = 1 + (a0 // 4) % 2
            pe.need(*free[b])
            if b == 1:
                pe.need(t_tab)
            for a in range(a0, a0 + n):
                r = P if a < NA - 1 else LAST
                pe.need(t_h[a])
                t = pe.mark(nc.tensor.transpose(bank[b][:, 128 * (a - a0):128 * (a - a0) + r], X[0:r, a, :],
                                                ident[0:r, 0:r]))
            act.need(t)
            w = min(N, 128 * (a0 + n)) - 128 * a0
            t = act.mark(nc.scalar.copy(Z[:, 0, 128 * a0:128 * a0 + w], bank[b][:, 0:w]))
            free[b] = [t]
        t_z0 = t
        dve.need(t_w)
        t_wr0 = dve.mark(nc.vector.tensor_scalar(wr[0][:, :, :], wr[0][:, :, :], 1.0 / S0, None, ALU.mult))
        for s in streams:
            s.need(t_flag, t_lo0, t_wr0, t_z0, t_tab, t_w)
        taken = nc.values_load(flag[0:1, 0:1], min_val=0, max_val=1)
        saved = [s.state() for s in streams]
        saved_slots = [s.n for s in slots]

        def rest(fast):
            free = {i: [] for i in range(8)}
            lin_banks = [7, 2]
            loops = [0]
            colfree = [[], [], []]
            agm_free = [[], []]
            rcb_free = [[], []]
            z_tok = {}
            NPART = {0: 128, 1: 256, 2: 128}

            if fast:
                sp.need(t_flag)
                t_rc = q_rc.mark(sp.eng.dma_start(rc_dram.rearrange("(j p k) -> p j k", j=NJ, k=GD), cntg[:, :, :]))
            else:
                with nc.allow_non_contiguous_dma(reason="general path"):
                    t_ed = q_tab.mark(sp.eng.dma_start(
                        ed, flat_pairs[0:NT * P, :].rearrange("(p t) two -> p t two", p=P)))
                for s in streams:
                    s.need(t_ed)
                t_rc = None
                nc.tensor.sem_inc(s_it["pe"], 1)

            def dump_parts(view, F):
                t = [s.last() for s in (act, dve)]
                sp.need(*t)
                for a0, a1, rows in ((0, NA - 1, P), (NA - 1, NA, LAST)):
                    tk = q_tab.mark(sp.eng.dma_start(
                        tab_dram[a0 * P:a0 * P + (a1 - a0) * rows, 0:2 * F].rearrange("(a p) f -> p a f", p=rows),
                        view[0:rows, a0:a1, :, :].rearrange("p a s f -> p a (s f)")))
                pool.need(tk)
                return tk

            def slow_block(c, F, banks, with_count):
                loops[0] += 1
                base = (loops[0] - 1) * NT
                nm = F // P
                for m in range(nm):
                    pe.need(*free[banks[m]])
                if with_count:
                    pe.need(*free[1])
                outs = [bank[banks[m]][:, 0:BD] for m in range(nm)] + ([bank[1][:, 0:BD]] if with_count else [])
                for o in outs:
                    nc.tensor.matmul(o, ones_h[:, :], zeros_h[:, :], start=True, stop=False, skip_group_check=True)
                G = onehot_d[:, 0:3, :].rearrange("p a b -> p (a b)")[:, 0:2 * F]
                O = onehot_s[:, 0:2, :].rearrange("p a b -> p (a b)")[:, 0:BD]
                with nc.Fori(0, NT) as i:
                    done = i + base
                    nc.gpsimd.wait_ge(s_it["pe"], done + 1)
                    nc.gpsimd.tensor_copy(slow_i[:, :], ed[:, bass.ds(i, 1), 0]).then_inc(s_it["idx"], 1)
                    nc.gpsimd.wait_ge(s_it["idx"], done + 1)
                    nc.gpsimd.sem_inc(s_it["go"])
                    nc.gpsimd.indirect_dma_start(
                        out=G, out_offset=None, in_=tab_rows(F),
                        in_offset=bass.IndirectOffsetOnAxis(ap=slow_i[:, 0:1], axis=0)).then_inc(s_g, 16)
                    nc.vector.wait_ge(s_it["pe"], done + 1)
                    nc.vector.tensor_scalar(slow_f[:, 0:1], ed[:, bass.ds(i, 1), 1], float(-BD * c), None,
                                            ALU.add).then_inc(s_it["col"], 1)
                    nc.vector.wait_ge(s_it["col"], done + 1)
                    nc.vector.tensor_scalar(O, iota[:, 0:BD], slow_f[:, 0:1], None,
                                            ALU.is_equal).then_inc(s_it["hot"], 1)
                    nc.tensor.wait_ge(s_it["hot"], done + 1)
                    nc.tensor.wait_ge(s_g, (done + 1) * 16)
                    for part in range(2):
                        for m in range(nm):
                            mm = nc.tensor.matmul(outs[m], G[:, part * F + m * P:part * F + m * P + P], O,
                                                  start=False, stop=False, skip_group_check=True)
                    if with_count:
                        mm = nc.tensor.matmul(outs[-1], ones_h[:, :], O, start=False, stop=False,
                                              skip_group_check=True)
                    mm.then_inc(s_it["pe"], 1)
                for o in outs:
                    t = pe.mark(nc.tensor.matmul(o, ones_h[:, :], zeros_h[:, :], start=False, stop=True,
                                                 skip_group_check=True))
                return t

            def tab_rows(F):
                return tab_dram.rearrange("r (h f) -> (r h) f", f=2 * F)[0:NA * P, :]

            def load_rc(c, layer):
                s = c % 2
                sp.need(t_rc, *rcb_free[s])
                return q_rcb[s].mark(sp.eng.dma_start(rcb[:, s, :],
                                                      rc_dram[BD * c:BD * c + BD].rearrange("(o n) -> o n", o=1)
                                                      .to_broadcast((P, BD))))

            def load_block(c):
                s = c % 3
                sp.need(t_blocks[c], *colfree[s])
                return q_blk[s].mark(sp.eng.dma_start(ring[:, s, :], C_dram[c, :, :]))

            def agg_mm(slot, view, F, m, a, part, b, first_, last_):
                r = P if a < NA - 1 else LAST
                mm = nc.tensor.matmul(bank[b][:, 0:BD], view[0:r, a, part, m * P:m * P + P],
                                      blk[slot][0:r, a, :], start=first_, stop=last_)
                return pe.mark(mm) if last_ else None

            def mean_of(c, nm, banks, t_agg, t_rcb, inv):
                s = c % 2
                dve.need(t_agg, t_rcb, *agm_free[s])
                for m in range(nm):
                    sc = inv if isinstance(inv, float) else inv[:, m:m + 1]
                    t = dve.mark(nc.vector.scalar_tensor_tensor(agm[:, s, m, :], bank[banks[m]][:, 0:BD], sc,
                                                                rcb[:, s, :], ALU.mult, ALU.mult))
                    free[banks[m]] = [t]
                rcb_free[s] = [t]
                return t

            def linear(c, layer, nk, t_mean):
                s = c % 2
                b = lin_banks[c % 2]
                pe.need(t_mean, *free[b])
                for m in range(2):
                    n = 0
                    for w, src in ((wl, agm[:, s, :, :]), (wr, Z[:, :, BD * c:BD * c + BD])):
                        for k in range(nk):
                            t = pe.mark(nc.tensor.matmul(bank[b][:, BD * m:BD * m + BD],
                                                         w[layer][:, k, m * P:m * P + P], src[:, k, :],
                                                         start=(n == 0), stop=(n == 2 * nk - 1)))
                            n += 1
                agm_free[s] = [t]
                act.need(t)
                for m in range(2):
                    t = act.mark(nc.scalar.activation(Z[:, m, BD * c:BD * c + BD], bank[b][:, BD * m:BD * m + BD],
                                                      ACT.Identity, bias=bias[layer][:, m:m + 1]))
                free[b] = [t]
                dve.need(t)
                for m in range(2):
                    t = dve.mark(nc.vector.bn_stats(st[:, m, c, :], Z[:, m, BD * c:BD * c + BD]))
                return t

            def batch_norm(layer):
                g, be = gamma[layer], beta[layer]
                w = lambda i: bnw[:, i, :]
                dve.need(dve.last())
                for m in range(2):
                    seq(dve, nc.vector.bn_aggr(mv[:, m, :], st[:, m, 0:NB, :]))
                act.need(dve.last())
                t = act.mark(nc.scalar.activation(w(0), mv[:, :, 1], ACT.Sqrt, bias=epsc[:, 0:1]))
                seq(dve, nc.vector.scalar_tensor_tensor(w(1), g, -1.0, g, ALU.mult, ALU.max))
                seq(dve, nc.vector.scalar_tensor_tensor(w(2), be, -1.0, be, ALU.mult, ALU.max))
                seq(dve, nc.vector.scalar_tensor_tensor(w(1), w(1), 1.01 * float(N) ** 0.5, w(2), ALU.mult, ALU.add))
                seq(dve, nc.vector.tensor_scalar(w(1), w(1), 1e-30, None, ALU.max))
                seq(dve, nc.vector.tensor_scalar(bnwi[:, 0, :], w(1).bitcast(I32), 0x7F800000, None,
                                                 ALU.bitwise_and))
                seq(dve, nc.vector.tensor_scalar(bnwi[:, 1, :], bnwi[:, 0, :], -1.0, float(268 << 23),
                                                 ALU.mult, ALU.add))
                s = bnwi[:, 1, :].bitcast(F32)
                seq(dve, nc.vector.tensor_scalar(w(8), bnwi[:, 0, :].bitcast(F32), 2.0 ** -14, None, ALU.mult))
                dve.need(t)
                seq(dve, nc.vector.reciprocal(w(3), w(0)))
                seq(dve, nc.vector.tensor_tensor(w(4), w(3), g, ALU.mult))
                seq(dve, nc.vector.tensor_tensor(w(5), mv[:, :, 0], w(4), ALU.mult))
                seq(dve, nc.vector.tensor_tensor(w(6), be, w(5), ALU.subtract))
                seq(dve, nc.vector.tensor_tensor(w(7), w(4), s, ALU.mult))
                seq(dve, nc.vector.tensor_tensor(w(6), w(6), s, ALU.mult))
                for k in range(2):
                    t = seq(dve, nc.vector.tensor_scalar(wr[layer + 1][:, k, :], wr[layer + 1][:, k, :],
                                                         w(8)[:, k:k + 1], None, ALU.mult))
                return t, w(7), w(6), w(8)

            def relu_cols(t_bn, sc, sh, c0, w):
                act.need(t_bn)
                for k in range(2):
                    t = act.mark(nc.scalar.activation(Z[:, k, c0:c0 + w], Z[:, k, c0:c0 + w], ACT.Relu,
                                                      bias=sh[:, k:k + 1], scale=sc[:, k:k + 1]))
                return t

            def split(b, view, a0, n, F, t_pe):
                full = n if a0 + n < NA else n - 1
                pieces = ([(P, 0, full)] if full else []) + ([(LAST, full, n)] if full < n else [])
                act.need(t_pe)
                src = lambda r, i, k: bank[b][0:r, i * F:k * F].rearrange("p (a f) -> p a f", a=k - i)
                for r, i, k in pieces:
                    t = act.mark(nc.scalar.copy(view[0:r, a0 + i:a0 + k, 0, :], src(r, i, k)))
                dve.need(t)
                for r, i, k in pieces:
                    t = dve.mark(nc.vector.tensor_tensor(view[0:r, a0 + i:a0 + k, 1, :], src(r, i, k),
                                                         view[0:r, a0 + i:a0 + k, 0, :], ALU.subtract))
                free[b] = [t]
                return t

            t_blocks = {}
            t_loaded = {}
            pend = None
            hot_free = [None] * NPB
            hot_n = [0]
            build_banks = [0, 1, 5, 6]
            if not fast:
                dump_parts(small, 128)

            def build_pair(c, i):
                b = build_banks[(c * PPB + i) % 4]
                pe.need(*free[b])
                for q in range(2):
                    g = c * GPB + 2 * i + q
                    j, p = divmod(g, P)
                    for h in range(2):
                        n = hot_n[0] % NPB
                        hot_n[0] += 1
                        dve.need(hot_free[n])
                        dve.mark(nc.vector.tensor_scalar(onehot_s[:, n, :], iota[:, 0:P], tab[:, j, 1, h, p:p + 1],
                                                         None, ALU.is_equal))
                        t = dve.mark(nc.vector.tensor_scalar(onehot_d[:, n, :], iota[:, 0:PW],
                                                             tab[:, j, 0, h, p:p + 1], None, ALU.is_equal))
                        pe.need(t)
                        t = pe.mark(nc.tensor.matmul(bank[b][:, NW * q:NW * q + NW], onehot_s[:, n, :],
                                                     onehot_d[:, n, 0:NW], start=(h == 0), stop=(h == 1)))
                        hot_free[n] = t
                act.need(t, *(colfree[c % 3] if i == 0 else []))
                t = act.mark(nc.scalar.copy(
                    blk[c % 3][:, :, 10 * i:10 * i + 10].rearrange("p a (q d) -> p a q d", q=2),
                    bank[b][:, 0:2 * NW].rearrange("p (q d a) -> p a q d", q=2, d=GD)))
                free[b] = [t]
                return t

            def store_block(c, t):
                s = c % 3
                sp.need(t)
                t_blocks[c] = q_st[s].mark(sp.eng.dma_start(C_dram[c, :, :], ring[:, s, :]))

            if fast:
                t_built = {}
                for c in range(NB + 1):
                    work = [(a, part) for a in range(NA) for part in range(2)]
                    if c >= 1:
                        b = 3 + (c - 1) % 2
                        t_rcb = load_rc(c - 1, 0)
                        pe.need(t_built[c - 1], *free[b])
                    done = 0
                    for i in range(PPB):
                        if c < NB:
                            t = build_pair(c, i)
                        if c >= 1:
                            upto = len(work) * (i + 1) // PPB
                            for a, part in work[done:upto]:
                                t_agg = agg_mm((c - 1) % 3, small, 128, 0, a, part, b, a == 0 and part == 0,
                                            a == NA - 1 and part == 1)
                            done = upto
                        if i == 4 and pend:
                            linear(pend[0], 0, 1, pend[1])
                            pend = None
                    if c < NB:
                        t_built[c] = t
                        store_block(c, t)
                    if c >= 1:
                        colfree[(c - 1) % 3] = [t_agg, t_blocks[c - 1]]
                        if pend:
                            linear(pend[0], 0, 1, pend[1])
                        pend = (c - 1, mean_of(c - 1, 1, [b], t_agg, t_rcb, 1.0 / S0))
                t_last = linear(pend[0], 0, 1, pend[1])
                pend = None
            else:
                for c in range(NB):
                    t = slow_block(c, 128, [3], True)
                    s = c % 2
                    dve.need(t, (q_rc.sem, q_rc.n), *rcb_free[s])
                    seq(dve, nc.vector.tensor_scalar(rcb[:, s, :], bank[1][:, 0:BD], 1.0, None, ALU.max))
                    free[1] = [dve.last()]
                    t_r = seq(dve, nc.vector.reciprocal(rcb[:, s, :], rcb[:, s, :]))
                    sp.need(t_r)
                    t_rc = q_rc.mark(sp.eng.dma_start(
                        rc_dram[BD * c:BD * c + BD].rearrange("(o n) -> o n", o=1), rcb[0:1, s, :]))
                    t_last = linear(c, 0, 1, mean_of(c, 1, [3], t, None, 1.0 / S0))
                for s in streams:
                    s.need(t_rc)

            t_bn, sc, sh, inv1 = batch_norm(0)
            ahead = 3
            if fast:
                for c in range(min(ahead, NB)):
                    t_loaded[c] = load_block(c)

            def prep1(t):
                a0 = 2 * t
                n = min(2, NA - a0)
                w = min(N, 128 * (a0 + n)) - 128 * a0
                b = [0, 1, 2][t % 3]
                t_r = relu_cols(t_bn, sc, sh, 128 * a0, w)
                pe.need(t_r, *free[b])
                for a in range(a0, a0 + n):
                    r = P if a < NA - 1 else LAST
                    for k in range(2):
                        tk = pe.mark(nc.tensor.transpose(bank[b][0:r, 256 * (a - a0) + 128 * k:256 * (a - a0) + 128 * k + 128],
                                                         Z[:, k, 128 * a:128 * a + r], ident))
                return split(b, wide, a0, n, 256, tk)

            npair = -(-NA // 2)
            if fast:
                pend = None
                for c in range(NB):
                    s = c % 3
                    bb = [(3, 4), (5, 6)][c % 2]
                    t_rcb = load_rc(c, 1)
                    if c == 0:
                        t_prep = prep1(0)
                    pe.need(t_loaded[c], *free[bb[0]], *free[bb[1]])
                    for t in range(npair):
                        if c == 0:
                            if t + 1 < npair:
                                nxt = prep1(t + 1)
                            pe.need(t_prep)
                            t_prep = nxt
                        for a in range(2 * t, min(2 * t + 2, NA)):
                            for part in range(2):
                                for m in range(2):
                                    t_agg = agg_mm(s, wide, 256, m, a, part, bb[m], a == 0 and part == 0,
                                                a == NA - 1 and part == 1)
                        if t == 3 and pend:
                            linear(pend[0], 1, 2, pend[1])
                            pend = None
                    colfree[s] = [t_agg]
                    if c + 3 < NB:
                        t_loaded[c + 3] = load_block(c + 3)
                    if pend:
                        linear(pend[0], 1, 2, pend[1])
                    pend = (c, mean_of(c, 2, bb, t_agg, t_rcb, inv1))
                t_last = linear(pend[0], 1, 2, pend[1])
                pend = None
            else:
                for t in range(npair):
                    prep1(t)
                dump_parts(wide, 256)
                for c in range(NB):
                    t_rcb = load_rc(c, 1)
                    t = slow_block(c, 256, [3, 4], False)
                    t_last = linear(c, 1, 2, mean_of(c, 2, [3, 4], t, t_rcb, inv1))

            t_bn, sc, sh, inv2 = batch_norm(1)
            for k in range(2):
                seq(dve, nc.vector.tensor_scalar(wl[2][:, k, :], wl[2][:, k, :], inv2[:, k:k + 1], None, ALU.mult))
            for k in range(2):
                seq(dve, nc.vector.scalar_tensor_tensor(spr[:, k, :], wl[2][:, k, :], -1.0, wl[2][:, k, :],
                                                        ALU.mult, ALU.max))
            pe.need(dve.last(), *free[0])
            for k in range(2):
                t = pe.mark(nc.tensor.matmul(bank[0][:, 0:P], ones[:, :], spr[:, k, :], start=(k == 0), stop=(k == 1)))
            dve.need(t)
            seq(dve, nc.vector.tensor_scalar(spr[:, 2, :], bank[0][:, 0:P], 2.0 ** 15 * 1.01, 1e-30, ALU.mult, ALU.max))
            free[0] = [dve.last()]
            seq(dve, nc.vector.tensor_scalar(spi[:, 0, :], spr[:, 2, :].bitcast(I32), 0x7F800000, None,
                                             ALU.bitwise_and))
            seq(dve, nc.vector.tensor_scalar(spi[:, 1, :], spi[:, 0, :], -1.0, float(268 << 23), ALU.mult, ALU.add))
            for k in range(2):
                seq(dve, nc.vector.tensor_tensor(wl[2][:, k, :], wl[2][:, k, :], spi[:, 1, :].bitcast(F32), ALU.mult))
            t_w2 = seq(dve, nc.vector.tensor_scalar(spr[:, 0, :], spi[:, 0, :].bitcast(F32), 2.0 ** -14, None,
                                                    ALU.mult))
            pe.need(t_w2, *free[0])
            t = pe.mark(nc.tensor.transpose(bank[0][:, 0:P], spr[:, 0, :], ident))
            dve.need(t)
            t_isp = seq(dve, nc.vector.tensor_copy(isp[:, :], bank[0][:, 0:1]))
            free[0] = [t_isp]

            if fast:
                for c in range(min(3, NB)):
                    t_loaded[c] = load_block(c)

            nquad = -(-NA // 4)

            def prep2(t):
                a0 = 4 * t
                n = min(4, NA - a0)
                w = min(N, 128 * (a0 + n)) - 128 * a0
                b = [0, 1, 2][t % 3]
                t_r = relu_cols(t_bn, sc, sh, 128 * a0, w)
                pe.need(t_r, *free[b])
                for a in range(a0, a0 + n):
                    r = P if a < NA - 1 else LAST
                    for k in range(2):
                        tk = pe.mark(nc.tensor.matmul(bank[b][0:r, 128 * (a - a0):128 * (a - a0) + 128],
                                                      Z[:, k, 128 * a:128 * a + r], wl[2][:, k, :],
                                                      start=(k == 0), stop=(k == 1)))
                return split(b, small, a0, n, 128, tk)

            sp.need(pe.last(), act.last(), dve.last(), t_last)
            for a0, a1, rows in ((0, NA - 1, P), (NA - 1, NA, LAST)):
                t_xr = q_xr.mark(sp.eng.dma_start(
                    xres[0:rows, a0:a1, :],
                    x[a0 * P:a0 * P + (a1 - a0) * rows, :].rearrange("(a p) f -> p a f", p=rows)))
            act.eng.preload_act_table_set("natural_log_exp_and_others")

            def linear2(c, t_mean):
                s = c % 2
                b = 7
                pe.need(*free[b])
                for k in range(2):
                    t = pe.mark(nc.tensor.matmul(bank[b][:, 0:BD], wr[2][:, k, :], Z[:, k, BD * c:BD * c + BD],
                                                 start=(k == 0), stop=(k == 1)))
                dve.need(t, t_mean)
                t = dve.mark(nc.vector.scalar_tensor_tensor(Z[:, 0, BD * c:BD * c + BD], bank[b][:, 0:BD],
                                                            bias[2][:, 0:1], agm[:, s, 0, :], ALU.add, ALU.add))
                free[b] = [t]
                agm_free[s] = [t]
                return t

            fin = [0, 0]
            o_tok = [None] * 4

            def final(t_z, upto):
                while fin[0] < NA:
                    a0 = fin[0]
                    n = min(2, NA - a0)
                    if a0 + n == NA and n == 2 and LAST < P:
                        n = 1
                    w = min(N, 128 * (a0 + n)) - 128 * a0
                    if 128 * a0 + w > upto:
                        return
                    r = P if a0 + n < NA else LAST
                    u = fin[1]
                    fin[0] += n
                    fin[1] += 1
                    b = [0, 1, 2][u % 3]
                    s = u % 4
                    pe.need(t_z, *free[b])
                    for i in range(n):
                        t = pe.mark(nc.tensor.transpose(bank[b][0:r, 128 * i:128 * i + 128],
                                                        Z[:, 0, 128 * (a0 + i):128 * (a0 + i) + r], ident))
                    v = bank[b][0:r, 0:128 * n].rearrange("p (a f) -> p a f", a=n)
                    dve.need(t, o_tok[s])
                    seq(dve, nc.vector.tensor_reduce(sm[0:r, 0, a0:a0 + n], v, AX.X, ALU.max))
                    t = seq(dve, nc.vector.tensor_tensor(dd[0:r, s, 0:n, :], v,
                                                         sm[0:r, 0, a0:a0 + n].unsqueeze(2).to_broadcast((r, n, P)),
                                                         ALU.subtract))
                    free[b] = [t]
                    act.need(t)
                    for i in range(n):
                        t = act.mark(nc.scalar.activation(ex[0:r, i, :], dd[0:r, s, i, :], ACT.Exp,
                                                          accum_out=sm[0:r, 1, a0 + i:a0 + i + 1]))
                    act.need(t)
                    t = act.mark(nc.scalar.activation(sm[0:r, 2, a0:a0 + n], sm[0:r, 1, a0:a0 + n], ACT.Ln))
                    dve.need(t, t_xr)
                    for i in range(n):
                        t = dve.mark(nc.vector.scalar_tensor_tensor(
                            dd[0:r, s, i, :], dd[0:r, s, i, :], sm[0:r, 2, a0 + i:a0 + i + 1], xres[0:r, a0 + i, :],
                            ALU.subtract, ALU.add))
                    sp.need(t)
                    o_tok[s] = q_o[s].mark(sp.eng.dma_start(
                        out[128 * a0:128 * a0 + (n - 1) * 128 + r, :].rearrange("(a p) f -> p a f", p=r),
                        dd[0:r, s, 0:n, :]))

            if fast:
                t_p = prep2(0)
                pend = None
                for c in range(NB):
                    s = c % 3
                    b = [3, 4][c % 2]
                    t_rcb = load_rc(c, 2)
                    pe.need(t_loaded[c], *free[b])
                    for t in range(nquad):
                        if c == 0:
                            nxt = prep2(t + 1) if t + 1 < nquad else None
                            pe.need(t_p)
                            t_p = nxt
                        for a in range(4 * t, min(4 * t + 4, NA)):
                            for part in range(2):
                                t_agg = agg_mm(s, small, 128, 0, a, part, b, a == 0 and part == 0,
                                            a == NA - 1 and part == 1)
                        if t == min(3, nquad - 1) and pend:
                            t_z = linear2(*pend)
                            pend = (c - 1, t_z)
                    colfree[s] = [t_agg]
                    if c + 3 < NB:
                        t_loaded[c + 3] = load_block(c + 3)
                    if pend:
                        final(pend[1], BD * c)
                    pend = (c, mean_of(c, 1, [b], t_agg, t_rcb, isp))
                final(linear2(*pend), N)
            else:
                for t in range(nquad):
                    prep2(t)
                dump_parts(small, 128)
                for c in range(NB):
                    t_rcb = load_rc(c, 2)
                    t = slow_block(c, 128, [3], False)
                    t_z = linear2(c, mean_of(c, 1, [3], t, t_rcb, isp))
                    final(t_z, BD * (c + 1))
            for t in o_tok + [(s.sem, s.n) for s in q_st + [q_rc, q_tab]]:
                if t and t[1]:
                    sp.need(t)

        with nc.If(taken):
            rest(True)
        with nc.Else():
            for s, v in zip(streams, saved):
                s.restore(v)
            for s, v in zip(slots, saved_slots):
                s.n = v
            rest(False)


def kernel(**inputs):
    import numpy as _np
    import concourse.bacc as _bacc
    from concourse import mybir as _mybir
    from concourse.bass_utils import run_bass_kernel_spmd as _run

    x = _np.ascontiguousarray(inputs["x"])
    src = _np.asarray(inputs["src"])
    dst = _np.asarray(inputs["dst"])
    N = x.shape[0]
    E = src.shape[0]
    R = -(-E // 256)
    EP = (R + 1) * 256
    pad = 2 * N + 1000
    NA = -(-N // 128)
    NJ = -(-(N // GD) // 128)
    pairs = _np.zeros((EP, 2), src.dtype)
    pairs[:, 1] = pad
    pairs[:E, 0] = src
    pairs[:E, 1] = dst
    dst_rows = _np.ascontiguousarray(pairs[:R * 256, 1].reshape(R, 256))
    const_f = _np.zeros((128, NJ + 128), _np.float32)
    const_f[:, :NJ] = GD * (_np.arange(NJ)[None, :] * 128 + _np.arange(128)[:, None])
    const_f[:, NJ:] = _np.eye(128)
    iota = _np.ascontiguousarray(_np.broadcast_to(_np.arange(256), (128, 256)).astype(_np.float16))

    def col(n):
        return _np.asarray(inputs["L0_gnn_" + n]).reshape(-1, 128).T

    vecs = _np.ascontiguousarray(_np.concatenate(
        [col(n) for n in ("bl0", "bl1", "bl2", "gamma0", "gamma1", "beta0", "beta1")], axis=1))
    arrays = {
        "x": x, "pairs": pairs.reshape(R + 1, 256, 2), "dst_rows": dst_rows,
        "samples": _np.ascontiguousarray(dst_rows[:, 0].reshape(1, R)),
        "const_f": const_f, "iota": iota, "vecs": vecs,
    }
    for i in range(3):
        for n in ("Wl", "Wr"):
            arrays[f"{n}T{i}"] = _np.ascontiguousarray(_np.asarray(inputs[f"L0_gnn_{n}{i}"]).T)

    nc = _bacc.Bacc("TRN2", target_bir_lowering=False, num_devices=1)
    named = {f"in_{k}_dram": v for k, v in arrays.items()}
    ap = {k: nc.dram_tensor(f"in_{k}_dram", v.shape, _mybir.dt.from_np(v.dtype), kind="ExternalInput").ap()
          for k, v in arrays.items()}
    out = nc.dram_tensor("out_0_dram", x.shape, _mybir.dt.from_np(x.dtype), kind="ExternalOutput").ap()
    gnn_program(nc, E, ap["x"], ap["pairs"], ap["dst_rows"], ap["samples"], ap["const_f"], ap["iota"],
                [ap[f"WlT{i}"] for i in range(3)], [ap[f"WrT{i}"] for i in range(3)], ap["vecs"], out)
    r = _run(nc, [named], core_ids=[0])
    return r.results[0]["out_0_dram"]
```

```python
from contextlib import ExitStack

import concourse.bass as bass
from concourse import mybir
from concourse.alu_op_type import AluOpType as ALU

F32 = mybir.dt.float32
F16 = mybir.dt.float16
I32 = mybir.dt.int32
U32 = mybir.dt.uint32
ACT = mybir.ActivationFunctionType
AX = mybir.AxisListType

P = 128
GD = 2
BD = 250
GPB = BD // GD
GPK = 5
GPS = 10
NST = -(-GPB // GPS)
EPS = 1e-5
S0 = 1024.0
NHOT = 3
NBT = 4
NTAB = 8


class Stream:

    def __init__(self, eng, sem):
        self.eng, self.sem, self.n, self.seen = eng, sem, 0, {}

    def mark(self, ins):
        ins.then_inc(self.sem, 1)
        self.n += 1
        return (self.sem, self.n)

    def last(self):
        return (self.sem, self.n)

    def need(self, *tokens):
        for t in tokens:
            if t is None:
                continue
            sem, val = t
            if self.seen.get(sem.name, 0) < val:
                self.eng.wait_ge(sem, val)
                self.seen[sem.name] = val

    def state(self):
        return self.n, dict(self.seen)

    def restore(self, s):
        self.n, self.seen = s[0], dict(s[1])


class Slot:

    def __init__(self, sem):
        self.sem, self.n = sem, 0

    def mark(self, ins):
        ins.then_inc(self.sem, 16)
        self.n += 16
        return (self.sem, self.n)


def gnn_program(nc, n_edges, x, pairs, dst_rows, samples, const_f, iota_h, WlT, WrT, vecs, out):
    N, F0 = x.shape
    E = n_edges
    EP = pairs.shape[0] * pairs.shape[1]
    R = dst_rows.shape[0]
    NA = -(-N // P)
    LAST = N - P * (NA - 1)
    NB = N // BD
    NT = -(-E // P)
    NW = GD * NA
    assert N % BD == 0 and NW <= P and GPK * NW <= 512 and NT * P <= EP

    flat_pairs = pairs.rearrange("r c two -> (r c) two")

    with ExitStack() as ctx:
        def sb(name, shape, dt=F32):
            return ctx.enter_context(nc.sbuf_tensor(name, shape, dt))

        def sem(name):
            return ctx.enter_context(nc.semaphore(name))

        C_dram = nc.dram_tensor("c_blocks", [NB, P, NA * BD], F16).ap()
        rc_dram = nc.dram_tensor("rc_row", [N], F32).ap()
        tab_dram = nc.dram_tensor("part_rows", [N * 512], F16).ap()

        bank = [ctx.enter_context(nc.psum_tensor(f"bank{i}", [P, 512], F32)) for i in range(8)]

        Z = sb("Z", [P, 2, NA * P])
        parts = sb("parts", [P, NA * 512], F16)
        ring = sb("ring", [P, 3, NA * BD], F16)
        agm = sb("agm", [P, 2, 2, BD])
        rcb = sb("rcb", [P, 2, BD])
        iotas = sb("iotas", [P, 4 * P], F16)
        iota = iotas[:, 0:2 * P]
        iota2 = iotas[:, 2 * P:4 * P].rearrange("p (x t) -> p x t", t=2)
        cf = sb("cf", [P, 2 * NB + P])
        thr = cf[:, 0:NB]
        thr_h = cf[:, NB:2 * NB]
        ident = cf[:, 2 * NB:2 * NB + P]
        wl = [sb("wl0", [P, 1, 256]), sb("wl1", [P, 2, 256]), sb("wl2", [P, 2, 128])]
        wr = [sb("wr0", [P, 1, 256]), sb("wr1", [P, 2, 256]), sb("wr2", [P, 2, 128])]
        vec = sb("vec", [P, 13])
        bias = [vec[:, 0:2], vec[:, 2:4], vec[:, 4:5]]
        gamma = [vec[:, 5:7], vec[:, 7:9]]
        beta = [vec[:, 9:11], vec[:, 11:13]]
        ones = sb("ones", [P, P])
        ones_h = sb("ones_h", [P, P], F16)
        zeros_h = sb("zeros_h", [P, BD], F16)
        s1 = sb("s1", [P, NB])
        s2 = sb("s2", [P, NB])
        row = sb("row", [P, NB])
        row_i = sb("row_i", [P, NB], U32)
        off = sb("off", [P, NB])
        first_i = sb("first_i", [P, NB], U32)
        sgn = sb("sgn", [P, NB, GD + 1])
        cut = sb("cut", [P, GD + 1])
        epsc = sb("epsc", [P, 1])
        cntg = sb("cntg", [P, NB, GD])
        smp_i = sb("smp_i", [P, R], I32)
        junk = sb("junk", [P, max(R, 4 * P)], F16)
        ex = junk[:, 0:4 * P].bitcast(F32).rearrange("p (a f) -> p a f", a=2)
        rows_i = sb("rows_i", [P, NBT, 256], I32)
        spr = rows_i[:, 0:2, :].rearrange("p s n -> p (s n)")[:, 0:3 * P].bitcast(F32).rearrange("p (a f) -> p a f", a=3)
        spi = rows_i[:, 2, :].rearrange("p (a f) -> p a f", a=2)
        dd = rows_i[:, 0:4, :].bitcast(F32).rearrange("p s (a f) -> p s a f", a=2)
        tot = sb("tot", [P, NB + 1])
        flag = sb("flag", [P, 1], I32)
        st = sb("st", [P, 2, max(NB, 25), 6])
        mv = sb("mv", [P, 2, 2])
        bnw = sb("bnw", [P, 12, 2])
        bnwi = sb("bnwi", [P, 2, 2], I32)
        mvx = sb("mvx", [P, NA, 6])
        rsx = sb("rsx", [P, 4, NA])
        isp = sb("isp", [P, 1])
        sm = sb("sm", [P, 4, NA])
        slow_f = sb("slow_f", [P, 2])
        slow_i = sb("slow_i", [P, 1], U32)

        small = parts[:, 0:NA * 256].rearrange("p (a s f) -> p a s f", a=NA, s=2)
        wide = parts[:, :].rearrange("p (a s f) -> p a s f", a=NA, s=2)
        upper = parts[:, NA * 256:NA * 512].bitcast(F32)
        xres = upper.rearrange("p (a f) -> p a f", a=NA)
        X = Z[:, 1, :].rearrange("p (a f) -> p a f", a=NA)
        HOT = GPS * (NW + P)
        need = NBT * 256 + NBT * 3 * P + NHOT * HOT // 2
        early = upper if NA * 128 >= need else sb("early", [P, need])
        win = early[:, 0:NBT * 256].bitcast(I32).rearrange("p (w n two) -> p w n two", w=NBT, two=2)
        wrk = early[:, NBT * 256:NBT * (256 + 3 * P)].rearrange("p (k n e) -> p k n e", k=3, e=P)
        hot = early[:, NBT * (256 + 3 * P):need].bitcast(F16).rearrange("p (s n) -> p s n", s=NHOT)
        tab = sb("tab", [P, NTAB, 2, P], F16)
        blk = [ring[:, s, :].rearrange("p (a d) -> p a d", a=NA) for s in range(3)]
        ed = ring[:, :, :].rearrange("p s n -> p (s n)").bitcast(I32)[:, 0:NT * 2] \
            .rearrange("p (t two) -> p t two", two=2)
        assert NT * 4 + 1024 <= 3 * NA * BD
        slow_g = ring[:, :, :].rearrange("p s n -> p (s n)")[:, NT * 4:NT * 4 + 512]
        slow_o = ring[:, :, :].rearrange("p s n -> p (s n)")[:, NT * 4 + 512:NT * 4 + 512 + BD]

        pe = Stream(nc.tensor, sem("s_pe"))
        dve = Stream(nc.vector, sem("s_dve"))
        act = Stream(nc.scalar, sem("s_act"))
        pool = Stream(nc.gpsimd, sem("s_pool"))
        sp = Stream(nc.sync, sem("s_sp"))
        streams = [pe, dve, act, pool, sp]
        q_c = Slot(sem("q_c"))
        q_x = [Slot(sem(f"q_x{i}")) for i in range(4)]
        q_w = Slot(sem("q_w"))
        q_row = [Slot(sem(f"q_row{j}")) for j in range(NBT)]
        q_win = [Slot(sem(f"q_win{j}")) for j in range(NBT)]
        q_rc = Slot(sem("q_rc"))
        q_blk = [Slot(sem(f"q_blk{i}")) for i in range(3)]
        q_st = [Slot(sem(f"q_st{i}")) for i in range(3)]
        q_rcb = [Slot(sem(f"q_rcb{i}")) for i in range(2)]
        q_xr = Slot(sem("q_xr"))
        q_o = [Slot(sem(f"q_o{i}")) for i in range(4)]
        q_tab = Slot(sem("q_tab"))
        s_g = sem("s_gather")
        s_it = {k: sem(f"s_it_{k}") for k in ("idx", "hot", "pe", "col", "go")}
        slots = [q_c, q_w, q_rc, q_xr, q_tab] + q_x + q_row + q_win + q_blk + q_st + q_rcb + q_o

        def seq(s, ins):
            t = s.mark(ins)
            s.need(t)
            return t

        free = {i: [] for i in range(8)}
        colfree = [[], [], []]
        agm_free = [[], []]
        rcb_free = [[], []]
        t_blocks = {}
        shared = (free, colfree, agm_free, rcb_free, t_blocks)
        lin_banks = [7, 2]

        cuts = [(NA - 1) * k // 4 for k in range(4)] + [NA]

        def load_x(k):
            for a0, a1, rows in ((cuts[k], min(cuts[k + 1], NA - 1), P), (NA - 1, cuts[k + 1], LAST)):
                if a0 < a1:
                    t = q_x[k].mark(sp.eng.dma_start(
                        X[0:rows, a0:a1, :],
                        x[a0 * P:a0 * P + (a1 - a0) * rows, :].rearrange("(a p) f -> p a f", p=rows)))
            return t

        q_c.mark(sp.eng.dma_start(smp_i[:, :], samples.to_broadcast((P, R))))
        q_c.mark(sp.eng.dma_start(cf[:, :], const_f))
        t_c = q_c.mark(sp.eng.dma_start(iotas[:, :], iota_h))
        t_x = [load_x(0), load_x(1)]

        for k in range(GD + 1):
            pool.mark(nc.gpsimd.memset(cut[:, k:k + 1], k - 0.5))
        pool.mark(nc.gpsimd.memset(ones[:, :], 1.0))
        pool.mark(nc.gpsimd.memset(ones_h[:, :], 1.0))
        pool.mark(nc.gpsimd.memset(epsc[:, :], EPS))
        pool.mark(nc.gpsimd.memset(mvx[:, NA - 1, :], 0.0))
        t_set = pool.mark(nc.gpsimd.memset(zeros_h[:, :], 0.0))

        t_tab = {}
        t_rc = {}
        win_free = [[] for _ in range(NBT)]
        tab_free = [[] for _ in range(NTAB)]
        row_free = [[] for _ in range(NBT)]
        last_junk = [None]
        wrk_free = [None]

        def count_below(src, c, width, into):
            act.need(last_junk[0])
            last_junk[0] = act.mark(nc.scalar.activation(junk[:, 0:width], src, ACT.Sign, bias=thr_h[:, c:c + 1],
                                                         scale=-1.0, accum_out=into))
            return last_junk[0]

        def table_chores(c0, c1):
            n = c1 - c0
            sl = slice(c0, c1)
            tok = {}
            dl, pen, hi = wrk[:, 0, 0:n, :], wrk[:, 1, 0:n, :], wrk[:, 2, 0:n, :].bitcast(I32)
            srcs = win[:, 0:n, :, 0]

            def samples_of(c):
                def do():
                    act.need(t_c)
                    tok["s1"] = count_below(smp_i[:, :], c, R, s1[:, c:c + 1])
                return do

            def rows_of():
                dve.need(tok["s1"])
                seq(dve, nc.vector.tensor_scalar(row[:, sl], s1[:, sl], 0.5, R / 2.0 - 1.0, ALU.mult, ALU.add))
                t = dve.mark(nc.vector.tensor_scalar(row_i[:, sl], row[:, sl], 0.0, None, ALU.max))
                pool.need(t)
                for c in range(c0, c1):
                    k = c - c0
                    pool.need(*row_free[k])
                    tok["row", c] = q_row[k].mark(nc.gpsimd.indirect_dma_start(
                        out=rows_i[:, k, :], out_offset=None, in_=dst_rows,
                        in_offset=bass.IndirectOffsetOnAxis(ap=row_i[:, c:c + 1], axis=0)))

            def in_row(c):
                def do():
                    act.need(tok["row", c])
                    tok["s2"] = count_below(rows_i[:, c - c0, :], c, 256, s2[:, c:c + 1])
                    row_free[c - c0] = [tok["s2"]]
                return do

            def windows():
                dve.need(tok["s2"])
                seq(dve, nc.vector.tensor_scalar(off[:, sl], s2[:, sl], 0.5, 128.0, ALU.mult, ALU.add))
                t = dve.mark(nc.vector.scalar_tensor_tensor(first_i[:, sl], row_i[:, sl], 256.0, off[:, sl],
                                                            ALU.mult, ALU.add))
                pool.need(t)
                for c in range(c0, c1):
                    w = c - c0
                    pool.need(*win_free[w])
                    tok["win", c] = q_win[w].mark(nc.gpsimd.indirect_dma_start(
                        out=win[:, w, :, :].rearrange("p n two -> p (n two)"), out_offset=None, in_=flat_pairs,
                        in_offset=bass.IndirectOffsetOnAxis(ap=first_i[:, c:c + 1], axis=0)))

            def from_first(c):
                def do():
                    w, k = c - c0, c - c0
                    dve.need(tok["win", c], wrk_free[0])
                    t = dve.mark(nc.vector.tensor_scalar(wrk[:, 0, k, :], win[:, w, :, 1], thr[:, c:c + 1], None,
                                                         ALU.subtract))
                    act.need(t, t_set)
                    for i in range(GD + 1):
                        act.need(last_junk[0])
                        last_junk[0] = act.mark(nc.scalar.activation(
                            junk[:, 0:P], wrk[:, 0, k, :], ACT.Sign, bias=cut[:, i:i + 1], scale=-1.0,
                            accum_out=sgn[:, c, i:i + 1]))
                    tok["sgn"] = last_junk[0]
                    tok["dl", c] = t
                return do

            def positions():
                pool.need(tok["dl", c1 - 1], tok["hi"])
                seq(pool, nc.gpsimd.tensor_scalar(pen, dl, GD - 0.5, 1000.0, ALU.is_ge, ALU.mult))
                tok["pen"] = seq(pool, nc.gpsimd.tensor_tensor(pen, pen, dl, ALU.add))

            def in_tile():
                dve.need(tok["dl", c1 - 1])
                tok["hi"] = seq(dve, nc.vector.tensor_scalar(hi, srcs, 7, None, ALU.logical_shift_right))

            def ready():
                dve.need(tok["pen"])
                seq(dve, nc.vector.scalar_tensor_tensor(pen, hi, float(GD), pen, ALU.mult, ALU.add))
                t = dve.mark(nc.vector.scalar_tensor_tensor(wrk[:, 2, 0:n, :], hi, -128.0, srcs, ALU.mult, ALU.add))
                tok["v"] = t
                for c in range(c0, c1):
                    win_free[c - c0] = [t]

            def turn(c):
                def do():
                    k, w = c - c0, c % NTAB
                    b = 4
                    pe.need(tok["v"], *free[b])
                    for i, j in ((0, 1), (1, 2)):
                        t = pe.mark(nc.tensor.transpose(bank[b][:, P * i:P * i + P], wrk[:, j, k, :], ident))
                    act.need(t, *tab_free[w])
                    t_tab[c] = act.mark(nc.scalar.copy(tab[:, w, :, :].rearrange("p v g -> p (v g)"),
                                                       bank[b][:, 0:2 * P]))
                    free[b] = [t_tab[c]]
                    wrk_free[0] = t
                return do

            def counts():
                dve.need(tok["sgn"])
                seq(dve, nc.vector.tensor_tensor(cntg[:, sl, :], sgn[:, sl, 1:GD + 1], sgn[:, sl, 0:GD], ALU.subtract))
                t = dve.mark(nc.vector.tensor_reduce(tot[:, c0:c0 + 1], cntg[:, sl, :], AX.XY, ALU.add))
                dve.need(t)
                seq(dve, nc.vector.tensor_scalar(cntg[:, sl, :], cntg[:, sl, :], 0.5, 1.0, ALU.mult, ALU.max))
                t = dve.mark(nc.vector.reciprocal(cntg[:, sl, :], cntg[:, sl, :]))
                sp.need(t)
                t = q_rc.mark(sp.eng.dma_start(
                    rc_dram[BD * c0:BD * c1].rearrange("(c p k) -> p c k", c=n, k=GD), cntg[0:GPB, sl, :]))
                sp.need(t)
                for c in range(c0, c1):
                    t_rc[c] = t

            def rest_():
                pass

            return {"tok": tok,
                    "samples": [samples_of(c) for c in range(c0, c1)],
                    "rows": [rows_of],
                    "windows": [in_row(c) for c in range(c0, c1)] + [windows],
                    "tables": [from_first(c) for c in range(c0, c1)] + [in_tile, positions, rest_, ready, rest_]
                    + [turn(c) for c in range(c0, c1)] + [counts],
                    "wait": [rest_] * 8}

        full = NA - 1
        groups = [(a0, min(4, full - a0), P) for a0 in range(0, full, 4)] + [(full, 1, LAST)]
        t_hi = {}
        t_lo = {}
        t_relu = {}

        def ln_stats(k, t_x):
            dve.need(t_x, t_set)
            for a in range(cuts[k], cuts[k + 1]):
                r = P if a < full else LAST
                dve.mark(nc.vector.bn_stats(mvx[0:r, a, :], X[0:r, a, :]))

        def ln_scales():
            dve.need(dve.last())
            col = lambda i: rsx[:, i, :]
            me, mo = mvx[:, :, 1], mvx[:, :, 4]
            dve.mark(nc.vector.tensor_tensor(col(0), me, mo, ALU.add))
            seq(dve, nc.vector.tensor_tensor(col(1), me, mo, ALU.subtract))
            dve.mark(nc.vector.tensor_tensor(col(2), mvx[:, :, 2], mvx[:, :, 5], ALU.add))
            seq(dve, nc.vector.tensor_tensor(col(1), col(1), col(1), ALU.mult))
            seq(dve, nc.vector.tensor_scalar(col(2), col(2), 1.0 / P, None, ALU.mult))
            t = seq(dve, nc.vector.scalar_tensor_tensor(col(2), col(1), 0.25, col(2), ALU.mult, ALU.add))
            act.need(t, t_set)
            t = act.mark(nc.scalar.activation(col(1), col(2), ACT.Sqrt, bias=epsc[:, 0:1]))
            dve.need(t)
            seq(dve, nc.vector.reciprocal(col(2), col(1)))
            seq(dve, nc.vector.tensor_scalar(col(2), col(2), S0, None, ALU.mult))
            return seq(dve, nc.vector.scalar_tensor_tensor(col(3), col(0), -0.5, col(2), ALU.mult, ALU.mult))

        def ln_relu(g, t_scales):
            a0, n, r = groups[g]
            act.need(t_scales)
            for a in range(a0, a0 + n):
                t_relu[g] = act.mark(nc.scalar.activation(X[0:r, a, :], X[0:r, a, :], ACT.Relu,
                                                          bias=rsx[0:r, 3, a:a + 1], scale=rsx[0:r, 2, a:a + 1]))

        def ln_parts(g):
            a0, n, r = groups[g]
            dve.need(t_relu[g])
            t_hi[g] = dve.mark(nc.vector.tensor_copy(small[0:r, a0:a0 + n, 0, :], X[0:r, a0:a0 + n, :]))
            pool.need(t_hi[g])
            t_lo[g] = pool.mark(nc.gpsimd.tensor_tensor(small[0:r, a0:a0 + n, 1, :], X[0:r, a0:a0 + n, :],
                                                        small[0:r, a0:a0 + n, 0, :], ALU.subtract))

        def ln_turn(g, b):
            a0, n, r = groups[g]
            pe.need(t_relu[g], *free[b])
            for a in range(a0, a0 + n):
                t = pe.mark(nc.tensor.transpose(bank[b][:, P * (a - a0):P * (a - a0) + r], X[0:r, a, :],
                                                ident[0:r, 0:r]))
            act.need(t)
            w = (n - 1) * P + r
            t = act.mark(nc.scalar.copy(Z[:, 0, P * a0:P * a0 + w], bank[b][:, 0:w]))
            free[b] = [t]
            return t

        def load_rc(c):
            s = c % 2
            sp.need(t_rc[c], *rcb_free[s])
            return q_rcb[s].mark(sp.eng.dma_start(
                rcb[:, s, :], rc_dram[BD * c:BD * c + BD].rearrange("(o n) -> o n", o=1).to_broadcast((P, BD))))

        def load_block(c):
            s = c % 3
            sp.need(t_blocks[c], *colfree[s])
            return q_blk[s].mark(sp.eng.dma_start(ring[:, s, :], C_dram[c, :, :]))

        def agg_mm(c, view, m, a, part, b):
            r = P if a < NA - 1 else LAST
            first, last = (a, part) == (0, 0), (a, part) == (NA - 1, 1)
            mm = nc.tensor.matmul(bank[b][:, 0:BD], view[0:r, a, part, m * P:m * P + P], blk[c % 3][0:r, a, :],
                                  start=first, stop=last)
            return pe.mark(mm) if last else None

        def mean_of(c, nm, banks, t_agg, t_rcb, inv):
            s = c % 2
            dve.need(t_agg, t_rcb, *agm_free[s])
            for m in range(nm):
                sc = inv if isinstance(inv, float) else inv[:, m:m + 1]
                t = dve.mark(nc.vector.scalar_tensor_tensor(agm[:, s, m, :], bank[banks[m]][:, 0:BD], sc,
                                                            rcb[:, s, :], ALU.mult, ALU.mult))
                free[banks[m]] = [t]
            rcb_free[s] = [t]
            return t

        def linear(c, layer, nk, t_mean, *t_h, banks=lin_banks):
            for do in linear_parts(c, layer, nk, t_mean, banks[c % 2], *t_h):
                t = do()
            return t

        def linear_parts(c, layer, nk, t_mean, b, *t_h):
            tok = {}
            zc = [Z[:, m, BD * c:BD * c + BD] for m in range(2)]

            def products():
                s = c % 2
                pe.need(t_mean, *t_h, *free[b])
                for m in range(2):
                    n = 0
                    for w, src in ((wr, Z[:, :, BD * c:BD * c + BD]), (wl, agm[:, s, :, :])):
                        for k in range(nk):
                            t = pe.mark(nc.tensor.matmul(bank[b][:, BD * m:BD * m + BD],
                                                         w[layer][:, k, m * P:m * P + P], src[:, k, :],
                                                         start=(n == 0), stop=(n == 2 * nk - 1)))
                            n += 1
                agm_free[s] = [t]
                tok["pe"] = t

            def biased():
                act.need(tok["pe"])
                for m in range(2):
                    t = act.mark(nc.scalar.activation(zc[m], bank[b][:, BD * m:BD * m + BD],
                                                      ACT.Identity, bias=bias[layer][:, m:m + 1]))
                free[b] = [t]
                tok["z"] = t

            def stats():
                dve.need(tok["z"])
                for m in range(2):
                    t = dve.mark(nc.vector.bn_stats(st[:, m, c, :], zc[m]))
                return t

            return [products, biased, stats]

        batches = [(0, 1)]
        while batches[-1][1] < NB:
            c0 = batches[-1][1]
            c1 = min(NB, c0 + NBT)
            batches.append((c0, c1))
        first = table_chores(*batches[0])
        second = table_chores(*batches[1])
        for chore in first["samples"] + first["rows"] + second["samples"]:
            chore()
        sp.need(first["tok"]["row", 0])
        t_x.append(load_x(2))
        ln_stats(0, t_x[0])
        ln_stats(1, t_x[1])
        for chore in first["windows"] + second["rows"]:
            chore()
        sp.need(first["tok"]["win", 0])
        t_x.append(load_x(3))
        for layer in range(3):
            for w, src in ((wl[layer], WlT[layer]), (wr[layer], WrT[layer])):
                q_w.mark(sp.eng.dma_start(w[:, :, :], src.rearrange("(k p) m -> p k m", p=P)))
        t_w = q_w.mark(sp.eng.dma_start(vec[:, :], vecs))
        for chore in first["tables"] + second["windows"]:
            chore()
        ln_stats(2, t_x[2])
        ln_stats(3, t_x[3])
        t_scales = ln_scales()
        dve.need(t_w)
        t_wr0 = dve.mark(nc.vector.tensor_scalar(wr[0][:, :, :], wr[0][:, :, :], 1.0 / S0, None, ALU.mult))
        hot_free = [[] for _ in range(NHOT)]
        build_banks = [0, 1, 5, 6]
        steps = [0]
        pending = []
        pending += second["tables"]
        todo = batches[2:]

        def build_step(c, i):
            n = min(GPS, GPB - GPS * i)
            q = (n + 1) // 2
            s = steps[0] % NHOT
            w = c % NTAB
            ps = hot[:, s, 0:GPS * NW].rearrange("p (q x t) -> p q x t", x=NW, t=2)
            bs = hot[:, s, GPS * NW:HOT].rearrange("p (q x t) -> p q x t", x=P, t=2)
            dve.need(t_tab[c], t_c, *hot_free[s])
            for v, o, x_ in ((1, bs, P), (0, ps, NW)):
                pos = tab[:, w, v, GPS * i:GPS * i + 2 * q].rearrange("p (q t) -> p q t", t=2)
                t = dve.mark(nc.vector.tensor_tensor(
                    o[:, 0:q, :, :], iota2[:, 0:x_, :].unsqueeze(1).to_broadcast((P, q, x_, 2)),
                    pos.unsqueeze(2).to_broadcast((P, q, x_, 2)), ALU.is_equal))
            tab_free[w] = [t]
            pe.need(t)
            for g0 in range(0, n, GPK):
                b = build_banks[(2 * steps[0] + g0 // GPK) % 4]
                pe.need(*free[b])
                for g in range(g0, g0 + GPK):
                    t = pe.mark(nc.tensor.matmul(bank[b][:, NW * (g - g0):NW * (g - g0) + NW],
                                                 bs[:, g // 2, :, g % 2], ps[:, g // 2, :, g % 2],
                                                 start=True, stop=True))
                hot_free[s] = [t]
                act.need(t, *(colfree[c % 3] if i == 0 else []))
                d0 = GD * (GPS * i + g0)
                t = act.mark(nc.scalar.copy(
                    blk[c % 3][:, :, d0:d0 + GD * GPK].rearrange("p a (g d) -> p a g d", d=GD),
                    bank[b][:, 0:GPK * NW].rearrange("p (g a d) -> p a g d", g=GPK, d=GD)))
                free[b] = [t]
            steps[0] += 1
            return t

        for c in range(NB + 1):
            if c < NB:
                while todo and todo[0][0] <= c + NBT and not pending:
                    made = table_chores(*todo.pop(0))
                    pending += [chore for k in ("samples", "rows", "wait", "windows", "wait", "tables") for chore in made[k]]
                left = max(1, (min([b0 for b0, _ in batches if b0 > c] + [10 ** 6]) - c)) * NST
                rate = -(-len(pending) // left)
            if c >= 1:
                work = [(a, part) for a in range(NA) for part in range(2)]
                b = (3, 2)[c % 2]
                t_rcb = load_rc(c - 1)
                pe.need(t_built, *free[b])
                done = 0
            for i in range(NST):
                if c < NB:
                    t = build_step(c, i)
                    for _ in range(min(rate, len(pending))):
                        pending.pop(0)()
                if c == 0:
                    for _ in range(-(-len(groups) // NST)):
                        if len(t_relu) < len(groups):
                            ln_relu(len(t_relu), t_scales)
                        if len(t_lo) + 1 < len(t_relu):
                            ln_parts(len(t_lo))
                if c >= 1:
                    upto = len(work) * (i + 1) // NST
                    for a, part in work[done:upto]:
                        if c == 1:
                            pe.need(t_lo[min(g for g, (a0, n, _) in enumerate(groups) if a < a0 + n)])
                        t_agg = agg_mm(c - 1, small, 0, a, part, b)
                    done = upto
                if c >= 2:
                    if i == 2:
                        act.need(t_hi[len(groups) - 1], t_lo[len(groups) - 1])
                        t_mean = mean_of(c - 2, 1, sums[0], sums[1], sums[2], 1.0 / S0)
                        parts_left = linear_parts(c - 2, 0, 1, t_mean, 7, t_h0, t_wr0)
                    elif i in (4, 6, 9):
                        parts_left.pop(0)()
                if c >= 1 and i == 10 and c <= len(groups):
                    t_h0 = ln_turn(c - 1, 7)
            if c == 0:
                while len(t_lo) < len(groups):
                    ln_parts(len(t_lo))
            if c < NB:
                t_built = t
                sp.need(t)
                t_blocks[c] = q_st[c % 3].mark(sp.eng.dma_start(C_dram[c, :, :], ring[:, c % 3, :]))
            if c >= 1:
                colfree[(c - 1) % 3] = [t_agg, t_blocks[c - 1]]
                sums = ([b], t_agg, t_rcb)
        t_l0 = linear(NB - 1, 0, 1, mean_of(NB - 1, 1, *sums, 1.0 / S0), t_h0, t_wr0)

        cols = [c0 for c0, _ in batches]
        dve.need(dve.last())
        seq(dve, nc.vector.tensor_copy(tot[:, NB:NB + 1], tot[:, cols[0]:cols[0] + 1]))
        for c0 in cols[1:]:
            seq(dve, nc.vector.tensor_tensor(tot[:, NB:NB + 1], tot[:, NB:NB + 1], tot[:, c0:c0 + 1], ALU.add))
        pe.need(dve.last(), t_set, *free[0])
        t = pe.mark(nc.tensor.matmul(bank[0][:, 0:1], ones[0:GPB, :], tot[0:GPB, NB:NB + 1], start=True, stop=True))
        dve.need(t)
        t_flag = dve.mark(nc.vector.tensor_scalar(flag[:, :], bank[0][:, 0:1], 2.0 * E, None, ALU.is_equal))
        free[0] = [t_flag]
        for s in streams:
            s.need(t_flag)
        taken = nc.values_load(flag[0:1, 0:1], min_val=0, max_val=1)

        def rest(fast):
            loops = [0]

            def tab_rows(F):
                return tab_dram[0:N * 2 * F].rearrange("(r f) -> r f", f=2 * F)

            def dump_parts(view, F, *made):
                sp.need(*made)
                for a0, a1, rows in ((0, NA - 1, P), (NA - 1, NA, LAST)):
                    tk = q_tab.mark(sp.eng.dma_start(
                        tab_rows(F)[a0 * P:a0 * P + (a1 - a0) * rows, :].rearrange("(a p) f -> p a f", p=rows),
                        view[0:rows, a0:a1, :, :].rearrange("p a s f -> p a (s f)")))
                pool.need(tk)

            def slow_block(c, F, banks, with_count):
                base = loops[0] * NT
                loops[0] += 1
                nm = F // P
                for m in range(nm):
                    pe.need(*free[banks[m]])
                if with_count:
                    pe.need(*free[1])
                outs = [bank[banks[m]][:, 0:BD] for m in range(nm)] + ([bank[1][:, 0:BD]] if with_count else [])
                for o in outs:
                    nc.tensor.matmul(o, ones_h[:, :], zeros_h[:, :], start=True, stop=False, skip_group_check=True)
                G = slow_g[:, 0:2 * F]
                with nc.Fori(0, NT) as i:
                    done = i + base
                    nc.gpsimd.wait_ge(s_it["pe"], done + 1)
                    nc.gpsimd.tensor_copy(slow_i[:, :], ed[:, bass.ds(i, 1), 0]).then_inc(s_it["idx"], 1)
                    nc.gpsimd.wait_ge(s_it["idx"], done + 1)
                    nc.gpsimd.sem_inc(s_it["go"])
                    nc.gpsimd.indirect_dma_start(
                        out=G, out_offset=None, in_=tab_rows(F),
                        in_offset=bass.IndirectOffsetOnAxis(ap=slow_i[:, 0:1], axis=0)).then_inc(s_g, 16)
                    nc.vector.wait_ge(s_it["pe"], done + 1)
                    nc.vector.tensor_scalar(slow_f[:, 0:1], ed[:, bass.ds(i, 1), 1], float(-BD * c), None,
                                            ALU.add).then_inc(s_it["col"], 1)
                    nc.vector.wait_ge(s_it["col"], done + 1)
                    nc.vector.tensor_scalar(slow_o, iota[:, 0:BD], slow_f[:, 0:1], None,
                                            ALU.is_equal).then_inc(s_it["hot"], 1)
                    nc.tensor.wait_ge(s_it["hot"], done + 1)
                    nc.tensor.wait_ge(s_g, (done + 1) * 16)
                    for part in range(2):
                        for m in range(nm):
                            mm = nc.tensor.matmul(outs[m], G[:, part * F + m * P:part * F + m * P + P], slow_o,
                                                  start=False, stop=False, skip_group_check=True)
                    if with_count:
                        mm = nc.tensor.matmul(outs[-1], ones_h[:, :], slow_o, start=False, stop=False,
                                              skip_group_check=True)
                    mm.then_inc(s_it["pe"], 1)
                for o in outs:
                    t = pe.mark(nc.tensor.matmul(o, ones_h[:, :], zeros_h[:, :], start=False, stop=True,
                                                 skip_group_check=True))
                return t

            if fast:
                t_end = t_l0
            else:
                for s in streams:
                    s.need(*[o.last() for o in streams if o.n], *[(o.sem, o.n) for o in slots if o.n])
                t_ed = q_tab.mark(sp.eng.dma_start(
                    ed, flat_pairs[0:NT * P, :].rearrange("(p t) two -> p t two", p=P)))
                for s in streams:
                    s.need(t_ed)
                nc.tensor.sem_inc(s_it["pe"], 1)
                for k in range(4):
                    ln_stats(k, load_x(k))
                t_scales = ln_scales()
                for g in range(len(groups)):
                    ln_relu(g, t_scales)
                    ln_parts(g)
                    h0 = ln_turn(g, (3, 7)[g % 2])
                lo0 = pool.last()
                dump_parts(small, 128, h0, lo0)
                for c in range(NB):
                    t = slow_block(c, 128, [3], True)
                    s = c % 2
                    dve.need(t, (q_rc.sem, q_rc.n), *rcb_free[s])
                    seq(dve, nc.vector.tensor_scalar(rcb[:, s, :], bank[1][:, 0:BD], 1.0, None, ALU.max))
                    free[1] = [dve.last()]
                    t_r = seq(dve, nc.vector.reciprocal(rcb[:, s, :], rcb[:, s, :]))
                    sp.need(t_r)
                    t_rc[c] = q_rc.mark(sp.eng.dma_start(
                        rc_dram[BD * c:BD * c + BD].rearrange("(o n) -> o n", o=1), rcb[0:1, s, :]))
                    t_end = linear(c, 0, 1, mean_of(c, 1, [3], t, None, 1.0 / S0), h0, lo0)
                for s in streams:
                    s.need(t_rc[NB - 1])

            def batch_norm(layer):
                g, be = gamma[layer], beta[layer]
                w = lambda i: bnw[:, i, :]
                dve.need(dve.last())
                for m in range(2):
                    seq(dve, nc.vector.bn_aggr(mv[:, m, :], st[:, m, 0:NB, :]))
                act.need(dve.last())
                t = act.mark(nc.scalar.activation(w(0), mv[:, :, 1], ACT.Sqrt, bias=epsc[:, 0:1]))
                seq(dve, nc.vector.scalar_tensor_tensor(w(1), g, -1.0, g, ALU.mult, ALU.max))
                seq(dve, nc.vector.scalar_tensor_tensor(w(2), be, -1.0, be, ALU.mult, ALU.max))
                seq(dve, nc.vector.scalar_tensor_tensor(w(1), w(1), 1.01 * float(N) ** 0.5, w(2), ALU.mult, ALU.add))
                seq(dve, nc.vector.tensor_scalar(w(1), w(1), 1e-30, None, ALU.max))
                seq(dve, nc.vector.tensor_scalar(bnwi[:, 0, :], w(1).bitcast(I32), 0x7F800000, None,
                                                 ALU.bitwise_and))
                seq(dve, nc.vector.tensor_scalar(bnwi[:, 1, :], bnwi[:, 0, :], -1.0, float(268 << 23),
                                                 ALU.mult, ALU.add))
                s = bnwi[:, 1, :].bitcast(F32)
                seq(dve, nc.vector.tensor_scalar(w(8), bnwi[:, 0, :].bitcast(F32), 2.0 ** -14, None, ALU.mult))
                dve.need(t)
                seq(dve, nc.vector.reciprocal(w(3), w(0)))
                seq(dve, nc.vector.tensor_tensor(w(4), w(3), g, ALU.mult))
                seq(dve, nc.vector.tensor_tensor(w(5), mv[:, :, 0], w(4), ALU.mult))
                seq(dve, nc.vector.tensor_tensor(w(6), be, w(5), ALU.subtract))
                seq(dve, nc.vector.tensor_tensor(w(7), w(4), s, ALU.mult))
                seq(dve, nc.vector.tensor_tensor(w(6), w(6), s, ALU.mult))
                for k in range(2):
                    t = seq(dve, nc.vector.tensor_scalar(wr[layer + 1][:, k, :], wr[layer + 1][:, k, :],
                                                         w(8)[:, k:k + 1], None, ALU.mult))
                return t, w(7), w(6), w(8)

            def relu_cols(t_bn, sc, sh, c0, w):
                act.need(t_bn)
                for k in range(2):
                    t = act.mark(nc.scalar.activation(Z[:, k, c0:c0 + w], Z[:, k, c0:c0 + w], ACT.Relu,
                                                      bias=sh[:, k:k + 1], scale=sc[:, k:k + 1]))
                return t

            def split(b, view, a0, n, F, t_pe):
                full = n if a0 + n < NA else n - 1
                pieces = ([(P, 0, full)] if full else []) + ([(LAST, full, n)] if full < n else [])
                act.need(t_pe)
                src = lambda r, i, k: bank[b][0:r, i * F:k * F].rearrange("p (a f) -> p a f", a=k - i)
                for r, i, k in pieces:
                    t = act.mark(nc.scalar.copy(view[0:r, a0 + i:a0 + k, 0, :], src(r, i, k)))
                dve.need(t)
                for r, i, k in pieces:
                    t = dve.mark(nc.vector.tensor_tensor(view[0:r, a0 + i:a0 + k, 1, :], src(r, i, k),
                                                         view[0:r, a0 + i:a0 + k, 0, :], ALU.subtract))
                free[b] = [t]
                return t

            t_loaded = {}
            t_bn, sc, sh, inv1 = batch_norm(0)
            ahead = 3
            if fast:
                for c in range(min(ahead, NB)):
                    t_loaded[c] = load_block(c)

            def prep1(t):
                a0 = 2 * t
                n = min(2, NA - a0)
                w = min(N, 128 * (a0 + n)) - 128 * a0
                b = [0, 1, 2][t % 3]
                t_r = relu_cols(t_bn, sc, sh, 128 * a0, w)
                pe.need(t_r, *free[b])
                for a in range(a0, a0 + n):
                    r = P if a < NA - 1 else LAST
                    for k in range(2):
                        tk = pe.mark(nc.tensor.transpose(bank[b][0:r, 256 * (a - a0) + 128 * k:256 * (a - a0) + 128 * k + 128],
                                                         Z[:, k, 128 * a:128 * a + r], ident))
                return split(b, wide, a0, n, 256, tk)

            npair = -(-NA // 2)
            if fast:
                pend = None
                for c in range(NB):
                    s = c % 3
                    bb = [(3, 4), (5, 6)][c % 2]
                    t_rcb = load_rc(c)
                    if c == 0:
                        t_prep = prep1(0)
                    pe.need(t_loaded[c], *free[bb[0]], *free[bb[1]])
                    for t in range(npair):
                        if c == 0:
                            if t + 1 < npair:
                                nxt = prep1(t + 1)
                            pe.need(t_prep)
                            t_prep = nxt
                        for a in range(2 * t, min(2 * t + 2, NA)):
                            for part in range(2):
                                for m in range(2):
                                    t_agg = agg_mm(c, wide, m, a, part, bb[m])
                        if t == 3 and pend:
                            linear(pend[0], 1, 2, pend[1])
                            pend = None
                    colfree[s] = [t_agg]
                    if c + 3 < NB:
                        t_loaded[c + 3] = load_block(c + 3)
                    if pend:
                        linear(pend[0], 1, 2, pend[1])
                    pend = (c, mean_of(c, 2, bb, t_agg, t_rcb, inv1))
                t_last = linear(pend[0], 1, 2, pend[1])
                pend = None
            else:
                for t in range(npair):
                    prep1(t)
                dump_parts(wide, 256, act.last(), dve.last())
                for c in range(NB):
                    t_rcb = load_rc(c)
                    t = slow_block(c, 256, [3, 4], False)
                    t_last = linear(c, 1, 2, mean_of(c, 2, [3, 4], t, t_rcb, inv1))

            t_bn, sc, sh, inv2 = batch_norm(1)
            for k in range(2):
                seq(dve, nc.vector.tensor_scalar(wl[2][:, k, :], wl[2][:, k, :], inv2[:, k:k + 1], None, ALU.mult))
            for k in range(2):
                seq(dve, nc.vector.scalar_tensor_tensor(spr[:, k, :], wl[2][:, k, :], -1.0, wl[2][:, k, :],
                                                        ALU.mult, ALU.max))
            pe.need(dve.last(), *free[0])
            for k in range(2):
                t = pe.mark(nc.tensor.matmul(bank[0][:, 0:P], ones[:, :], spr[:, k, :], start=(k == 0), stop=(k == 1)))
            dve.need(t)
            seq(dve, nc.vector.tensor_scalar(spr[:, 2, :], bank[0][:, 0:P], 2.0 ** 15 * 1.01, 1e-30, ALU.mult, ALU.max))
            free[0] = [dve.last()]
            seq(dve, nc.vector.tensor_scalar(spi[:, 0, :], spr[:, 2, :].bitcast(I32), 0x7F800000, None,
                                             ALU.bitwise_and))
            seq(dve, nc.vector.tensor_scalar(spi[:, 1, :], spi[:, 0, :], -1.0, float(268 << 23), ALU.mult, ALU.add))
            for k in range(2):
                seq(dve, nc.vector.tensor_tensor(wl[2][:, k, :], wl[2][:, k, :], spi[:, 1, :].bitcast(F32), ALU.mult))
            t_w2 = seq(dve, nc.vector.tensor_scalar(spr[:, 0, :], spi[:, 0, :].bitcast(F32), 2.0 ** -14, None,
                                                    ALU.mult))
            pe.need(t_w2, *free[0])
            t = pe.mark(nc.tensor.transpose(bank[0][:, 0:P], spr[:, 0, :], ident))
            dve.need(t)
            t_isp = seq(dve, nc.vector.tensor_copy(isp[:, :], bank[0][:, 0:1]))
            free[0] = [t_isp]

            if fast:
                for c in range(min(3, NB)):
                    t_loaded[c] = load_block(c)

            nquad = -(-NA // 4)

            def prep2(t):
                a0 = 4 * t
                n = min(4, NA - a0)
                w = min(N, 128 * (a0 + n)) - 128 * a0
                b = [0, 1, 2][t % 3]
                t_r = relu_cols(t_bn, sc, sh, 128 * a0, w)
                pe.need(t_r, *free[b])
                for a in range(a0, a0 + n):
                    r = P if a < NA - 1 else LAST
                    for k in range(2):
                        tk = pe.mark(nc.tensor.matmul(bank[b][0:r, 128 * (a - a0):128 * (a - a0) + 128],
                                                      Z[:, k, 128 * a:128 * a + r], wl[2][:, k, :],
                                                      start=(k == 0), stop=(k == 1)))
                return split(b, small, a0, n, 128, tk)

            sp.need(pe.last(), act.last(), dve.last(), t_last)
            for a0, a1, rows in ((0, NA - 1, P), (NA - 1, NA, LAST)):
                t_xr = q_xr.mark(sp.eng.dma_start(
                    xres[0:rows, a0:a1, :],
                    x[a0 * P:a0 * P + (a1 - a0) * rows, :].rearrange("(a p) f -> p a f", p=rows)))
            act.eng.preload_act_table_set("natural_log_exp_and_others")

            def linear2(c, t_mean):
                s = c % 2
                b = 7
                pe.need(*free[b])
                for k in range(2):
                    t = pe.mark(nc.tensor.matmul(bank[b][:, 0:BD], wr[2][:, k, :], Z[:, k, BD * c:BD * c + BD],
                                                 start=(k == 0), stop=(k == 1)))
                dve.need(t, t_mean)
                t = dve.mark(nc.vector.scalar_tensor_tensor(Z[:, 0, BD * c:BD * c + BD], bank[b][:, 0:BD],
                                                            bias[2][:, 0:1], agm[:, s, 0, :], ALU.add, ALU.add))
                free[b] = [t]
                agm_free[s] = [t]
                return t

            fin = [0, 0]
            o_tok = [None] * 4

            def final(t_z, upto):
                while fin[0] < NA:
                    a0 = fin[0]
                    n = min(2, NA - a0)
                    if a0 + n == NA and n == 2 and LAST < P:
                        n = 1
                    w = min(N, 128 * (a0 + n)) - 128 * a0
                    if 128 * a0 + w > upto:
                        return
                    r = P if a0 + n < NA else LAST
                    u = fin[1]
                    fin[0] += n
                    fin[1] += 1
                    b = [0, 1, 2][u % 3]
                    s = u % 4
                    pe.need(t_z, *free[b])
                    for i in range(n):
                        t = pe.mark(nc.tensor.transpose(bank[b][0:r, 128 * i:128 * i + 128],
                                                        Z[:, 0, 128 * (a0 + i):128 * (a0 + i) + r], ident))
                    v = bank[b][0:r, 0:128 * n].rearrange("p (a f) -> p a f", a=n)
                    dve.need(t, o_tok[s])
                    seq(dve, nc.vector.tensor_reduce(sm[0:r, 0, a0:a0 + n], v, AX.X, ALU.max))
                    t = seq(dve, nc.vector.tensor_tensor(dd[0:r, s, 0:n, :], v,
                                                         sm[0:r, 0, a0:a0 + n].unsqueeze(2).to_broadcast((r, n, P)),
                                                         ALU.subtract))
                    free[b] = [t]
                    act.need(t)
                    for i in range(n):
                        t = act.mark(nc.scalar.activation(ex[0:r, i, :], dd[0:r, s, i, :], ACT.Exp,
                                                          accum_out=sm[0:r, 1, a0 + i:a0 + i + 1]))
                    act.need(t)
                    t = act.mark(nc.scalar.activation(sm[0:r, 2, a0:a0 + n], sm[0:r, 1, a0:a0 + n], ACT.Ln))
                    dve.need(t, t_xr)
                    for i in range(n):
                        t = dve.mark(nc.vector.scalar_tensor_tensor(
                            dd[0:r, s, i, :], dd[0:r, s, i, :], sm[0:r, 2, a0 + i:a0 + i + 1], xres[0:r, a0 + i, :],
                            ALU.subtract, ALU.add))
                    sp.need(t)
                    o_tok[s] = q_o[s].mark(sp.eng.dma_start(
                        out[128 * a0:128 * a0 + (n - 1) * 128 + r, :].rearrange("(a p) f -> p a f", p=r),
                        dd[0:r, s, 0:n, :]))

            if fast:
                t_p = prep2(0)
                pend = None
                for c in range(NB):
                    s = c % 3
                    b = [3, 4][c % 2]
                    t_rcb = load_rc(c)
                    pe.need(t_loaded[c], *free[b])
                    for t in range(nquad):
                        if c == 0:
                            nxt = prep2(t + 1) if t + 1 < nquad else None
                            pe.need(t_p)
                            t_p = nxt
                        for a in range(4 * t, min(4 * t + 4, NA)):
                            for part in range(2):
                                t_agg = agg_mm(c, small, 0, a, part, b)
                        if t == min(3, nquad - 1) and pend:
                            t_z = linear2(*pend)
                            pend = (c - 1, t_z)
                    colfree[s] = [t_agg]
                    if c + 3 < NB:
                        t_loaded[c + 3] = load_block(c + 3)
                    if pend:
                        final(pend[1], BD * c)
                    pend = (c, mean_of(c, 1, [b], t_agg, t_rcb, isp))
                final(linear2(*pend), N)
            else:
                for t in range(nquad):
                    prep2(t)
                dump_parts(small, 128, act.last(), dve.last())
                for c in range(NB):
                    t_rcb = load_rc(c)
                    t = slow_block(c, 128, [3], False)
                    t_z = linear2(c, mean_of(c, 1, [3], t, t_rcb, isp))
                    final(t_z, BD * (c + 1))
            for t in o_tok + [(s.sem, s.n) for s in q_st + [q_rc, q_tab]]:
                if t and t[1]:
                    sp.need(t)

        kept = ([s.state() for s in streams], [s.n for s in slots], {k: list(v) for k, v in free.items()},
                [list(v) for v in agm_free], [list(v) for v in rcb_free])
        with nc.If(taken):
            rest(True)
        with nc.Else():
            for s, v in zip(streams, kept[0]):
                s.restore(v)
            for s, v in zip(slots, kept[1]):
                s.n = v
            free.update(kept[2])
            agm_free[:], rcb_free[:] = kept[3], kept[4]
            rest(False)


def kernel(**inputs):
    import numpy as _np
    import concourse.bacc as _bacc
    from concourse import mybir as _mybir
    from concourse.bass_utils import run_bass_kernel_spmd as _run

    x = _np.ascontiguousarray(inputs["x"])
    src = _np.asarray(inputs["src"])
    dst = _np.asarray(inputs["dst"])
    N = x.shape[0]
    E = src.shape[0]
    R = -(-E // 256)
    EP = (R + 1) * 256
    pad = 2 * N + 1000
    NA = -(-N // 128)
    NB = N // BD
    pairs = _np.zeros((EP, 2), src.dtype)
    pairs[:, 1] = pad
    pairs[:E, 0] = src
    pairs[:E, 1] = dst
    dst_rows = _np.ascontiguousarray(pairs[:R * 256, 1].reshape(R, 256))
    const_f = _np.zeros((128, 2 * NB + 128), _np.float32)
    const_f[:, :NB] = BD * _np.arange(NB)[None, :] + GD * _np.arange(128)[:, None]
    const_f[:, NB:2 * NB] = const_f[:, :NB] - 0.5
    const_f[:, 2 * NB:] = _np.eye(128)
    iota = _np.zeros((128, 512), _np.float16)
    iota[:, :256] = _np.arange(256)
    iota[:, 256:] = _np.repeat(_np.arange(128), 2)

    def col(n):
        return _np.asarray(inputs["L0_gnn_" + n]).reshape(-1, 128).T

    vecs = _np.ascontiguousarray(_np.concatenate(
        [col(n) for n in ("bl0", "bl1", "bl2", "gamma0", "gamma1", "beta0", "beta1")], axis=1))
    arrays = {
        "x": x, "pairs": pairs.reshape(R + 1, 256, 2), "dst_rows": dst_rows,
        "samples": _np.ascontiguousarray(dst_rows[:, 0].reshape(1, R)),
        "const_f": const_f, "iota": iota, "vecs": vecs,
    }
    for i in range(3):
        for n in ("Wl", "Wr"):
            arrays[f"{n}T{i}"] = _np.ascontiguousarray(_np.asarray(inputs[f"L0_gnn_{n}{i}"]).T)

    nc = _bacc.Bacc("TRN2", target_bir_lowering=False, num_devices=1)
    named = {f"in_{k}_dram": v for k, v in arrays.items()}
    ap = {k: nc.dram_tensor(f"in_{k}_dram", v.shape, _mybir.dt.from_np(v.dtype), kind="ExternalInput").ap()
          for k, v in arrays.items()}
    out = nc.dram_tensor("out_0_dram", x.shape, _mybir.dt.from_np(x.dtype), kind="ExternalOutput").ap()
    gnn_program(nc, E, ap["x"], ap["pairs"], ap["dst_rows"], ap["samples"], ap["const_f"], ap["iota"],
                [ap[f"WlT{i}"] for i in range(3)], [ap[f"WrT{i}"] for i in range(3)], ap["vecs"], out)
    r = _run(nc, [named], core_ids=[0])
    return r.results[0]["out_0_dram"]
```

```python
from contextlib import ExitStack

import concourse.bass as bass
from concourse import mybir
from concourse.alu_op_type import AluOpType as ALU

F32 = mybir.dt.float32
F16 = mybir.dt.float16
I32 = mybir.dt.int32
U32 = mybir.dt.uint32
ACT = mybir.ActivationFunctionType
AX = mybir.AxisListType

P = 128
GD = 2
BD = 250
GPB = BD // GD
GPK = 5
GPS = 10
NST = -(-GPB // GPS)
EPS = 1e-5
S0 = 1024.0
NHOT = 3
NBT = 4
NTAB = 8


class Stream:

    def __init__(self, eng, sem):
        self.eng, self.sem, self.n, self.seen = eng, sem, 0, {}

    def mark(self, ins):
        ins.then_inc(self.sem, 1)
        self.n += 1
        return (self.sem, self.n)

    def last(self):
        return (self.sem, self.n)

    def need(self, *tokens):
        for t in tokens:
            if t is None:
                continue
            sem, val = t
            if self.seen.get(sem.name, 0) < val:
                self.eng.wait_ge(sem, val)
                self.seen[sem.name] = val

    def state(self):
        return self.n, dict(self.seen)

    def restore(self, s):
        self.n, self.seen = s[0], dict(s[1])


class Slot:

    def __init__(self, sem):
        self.sem, self.n = sem, 0

    def mark(self, ins):
        ins.then_inc(self.sem, 16)
        self.n += 16
        return (self.sem, self.n)


def gnn_program(nc, n_edges, x, pairs, dst_rows, samples, const_f, iota_h, WlT, WrT, vecs, out):
    N, F0 = x.shape
    E = n_edges
    EP = pairs.shape[0] * pairs.shape[1]
    R = dst_rows.shape[0]
    NA = -(-N // P)
    LAST = N - P * (NA - 1)
    NB = N // BD
    NT = -(-E // P)
    NW = GD * NA
    assert N % BD == 0 and NW <= P and GPK * NW <= 512 and NT * P <= EP

    flat_pairs = pairs.rearrange("r c two -> (r c) two")

    with ExitStack() as ctx:
        def sb(name, shape, dt=F32):
            return ctx.enter_context(nc.sbuf_tensor(name, shape, dt))

        def sem(name):
            return ctx.enter_context(nc.semaphore(name))

        C_dram = nc.dram_tensor("c_blocks", [NB, P, NA * BD], F16).ap()
        rc_dram = nc.dram_tensor("rc_row", [N], F32).ap()
        tab_dram = nc.dram_tensor("part_rows", [N * 512], F16).ap()

        bank = [ctx.enter_context(nc.psum_tensor(f"bank{i}", [P, 512], F32)) for i in range(8)]

        Z = sb("Z", [P, 2, NA * P])
        parts = sb("parts", [P, NA * 512], F16)
        ring = sb("ring", [P, 3, NA * BD], F16)
        agm = sb("agm", [P, 2, 2, BD])
        rcb = sb("rcb", [P, 2, BD])
        iotas = sb("iotas", [P, 4 * P], F16)
        iota = iotas[:, 0:2 * P]
        iota2 = iotas[:, 2 * P:4 * P].rearrange("p (x t) -> p x t", t=2)
        cf = sb("cf", [P, 2 * NB + P])
        thr = cf[:, 0:NB]
        thr_h = cf[:, NB:2 * NB]
        ident = cf[:, 2 * NB:2 * NB + P]
        wl = [sb("wl0", [P, 1, 256]), sb("wl1", [P, 2, 256]), sb("wl2", [P, 2, 128])]
        wr = [sb("wr0", [P, 1, 256]), sb("wr1", [P, 2, 256]), sb("wr2", [P, 2, 128])]
        vec = sb("vec", [P, 13])
        bias = [vec[:, 0:2], vec[:, 2:4], vec[:, 4:5]]
        gamma = [vec[:, 5:7], vec[:, 7:9]]
        beta = [vec[:, 9:11], vec[:, 11:13]]
        ones = sb("ones", [P, P])
        ones_h = sb("ones_h", [P, P], F16)
        zeros_h = sb("zeros_h", [P, BD], F16)
        s1 = sb("s1", [P, NB])
        s2 = sb("s2", [P, NB])
        row = sb("row", [P, NB])
        row_i = sb("row_i", [P, NB], U32)
        off = sb("off", [P, NB])
        first_i = sb("first_i", [P, NB], U32)
        sgn = sb("sgn", [P, NB, GD + 1])
        cut = sb("cut", [P, GD + 1])
        epsc = sb("epsc", [P, 1])
        cntg = sb("cntg", [P, NB, GD])
        smp_i = sb("smp_i", [P, R], I32)
        junk = sb("junk", [P, max(R, 4 * P)], F16)
        ex = junk[:, 0:4 * P].bitcast(F32).rearrange("p (a f) -> p a f", a=2)
        rows_i = sb("rows_i", [P, NBT, 256], I32)
        spr = rows_i[:, 0:2, :].rearrange("p s n -> p (s n)")[:, 0:3 * P].bitcast(F32).rearrange("p (a f) -> p a f", a=3)
        spi = rows_i[:, 2, :].rearrange("p (a f) -> p a f", a=2)
        dd = rows_i[:, 0:4, :].bitcast(F32).rearrange("p s (a f) -> p s a f", a=2)
        tot = sb("tot", [P, NB + 1])
        flag = sb("flag", [P, 1], I32)
        st = sb("st", [P, 2, max(NB, 25), 6])
        mv = sb("mv", [P, 2, 2])
        bnw = sb("bnw", [P, 2, 6, 2])
        bnt = sb("bnt", [P, 3, 2])
        mvx = sb("mvx", [P, NA, 6])
        rsx = sb("rsx", [P, 4, NA])
        isp = sb("isp", [P, 1])
        sm = sb("sm", [P, 4, NA])
        slow_f = sb("slow_f", [P, 2])
        slow_i = sb("slow_i", [P, 1], U32)

        small = parts[:, 0:NA * 256].rearrange("p (a s f) -> p a s f", a=NA, s=2)
        wide = parts[:, :].rearrange("p (a s f) -> p a s f", a=NA, s=2)
        upper = parts[:, NA * 256:NA * 512].bitcast(F32)
        xres = upper.rearrange("p (a f) -> p a f", a=NA)
        X = Z[:, 1, :].rearrange("p (a f) -> p a f", a=NA)
        HOT = GPS * (NW + P)
        need = NBT * 256 + NBT * 3 * P + NHOT * HOT // 2
        early = upper if NA * 128 >= need else sb("early", [P, need])
        win = early[:, 0:NBT * 256].bitcast(I32).rearrange("p (w n two) -> p w n two", w=NBT, two=2)
        wrk = early[:, NBT * 256:NBT * (256 + 3 * P)].rearrange("p (k n e) -> p k n e", k=3, e=P)
        hot = early[:, NBT * (256 + 3 * P):need].bitcast(F16).rearrange("p (s n) -> p s n", s=NHOT)
        tab = sb("tab", [P, NTAB, 2, P], F16)
        blk = [ring[:, s, :].rearrange("p (a d) -> p a d", a=NA) for s in range(3)]
        ed = ring[:, :, :].rearrange("p s n -> p (s n)").bitcast(I32)[:, 0:NT * 2] \
            .rearrange("p (t two) -> p t two", two=2)
        assert NT * 4 + 1024 <= 3 * NA * BD
        slow_g = ring[:, :, :].rearrange("p s n -> p (s n)")[:, NT * 4:NT * 4 + 512]
        slow_o = ring[:, :, :].rearrange("p s n -> p (s n)")[:, NT * 4 + 512:NT * 4 + 512 + BD]

        pe = Stream(nc.tensor, sem("s_pe"))
        dve = Stream(nc.vector, sem("s_dve"))
        act = Stream(nc.scalar, sem("s_act"))
        pool = Stream(nc.gpsimd, sem("s_pool"))
        sp = Stream(nc.sync, sem("s_sp"))
        streams = [pe, dve, act, pool, sp]
        q_c = Slot(sem("q_c"))
        q_x = [Slot(sem(f"q_x{i}")) for i in range(4)]
        q_w = Slot(sem("q_w"))
        q_row = [Slot(sem(f"q_row{j}")) for j in range(NBT)]
        q_win = [Slot(sem(f"q_win{j}")) for j in range(NBT)]
        q_rc = Slot(sem("q_rc"))
        q_blk = [Slot(sem(f"q_blk{i}")) for i in range(3)]
        q_st = [Slot(sem(f"q_st{i}")) for i in range(3)]
        q_rcb = [Slot(sem(f"q_rcb{i}")) for i in range(2)]
        q_xr = Slot(sem("q_xr"))
        q_o = [Slot(sem(f"q_o{i}")) for i in range(4)]
        q_tab = Slot(sem("q_tab"))
        s_g = sem("s_gather")
        s_it = {k: sem(f"s_it_{k}") for k in ("idx", "hot", "pe", "col", "go")}
        slots = [q_c, q_w, q_rc, q_xr, q_tab] + q_x + q_row + q_win + q_blk + q_st + q_rcb + q_o

        def seq(s, ins):
            t = s.mark(ins)
            s.need(t)
            return t

        free = {i: [] for i in range(8)}
        colfree = [[], [], []]
        agm_free = [[], []]
        rcb_free = [[], []]
        t_blocks = {}
        t_loaded = {}
        lin_banks = [7, 2]

        cuts = [(NA - 1) * k // 4 for k in range(4)] + [NA]

        def load_x(k):
            for a0, a1, rows in ((cuts[k], min(cuts[k + 1], NA - 1), P), (NA - 1, cuts[k + 1], LAST)):
                if a0 < a1:
                    t = q_x[k].mark(sp.eng.dma_start(
                        X[0:rows, a0:a1, :],
                        x[a0 * P:a0 * P + (a1 - a0) * rows, :].rearrange("(a p) f -> p a f", p=rows)))
            return t

        q_c.mark(sp.eng.dma_start(smp_i[:, :], samples.to_broadcast((P, R))))
        q_c.mark(sp.eng.dma_start(cf[:, :], const_f))
        t_c = q_c.mark(sp.eng.dma_start(iotas[:, :], iota_h))
        t_x = [load_x(0), load_x(1)]

        for k in range(GD + 1):
            pool.mark(nc.gpsimd.memset(cut[:, k:k + 1], k - 0.5))
        pool.mark(nc.gpsimd.memset(ones[:, :], 1.0))
        pool.mark(nc.gpsimd.memset(ones_h[:, :], 1.0))
        pool.mark(nc.gpsimd.memset(epsc[:, :], EPS))
        pool.mark(nc.gpsimd.memset(mvx[:, NA - 1, :], 0.0))
        t_set = pool.mark(nc.gpsimd.memset(zeros_h[:, :], 0.0))

        t_tab = {}
        t_rc = {}
        win_free = [[] for _ in range(NBT)]
        tab_free = [[] for _ in range(NTAB)]
        row_free = [[] for _ in range(NBT)]
        last_junk = [None]
        wrk_free = [None, None]

        def count_below(src, c, width, into):
            act.need(last_junk[0])
            last_junk[0] = act.mark(nc.scalar.activation(junk[:, 0:width], src, ACT.Sign, bias=thr_h[:, c:c + 1],
                                                         scale=-1.0, accum_out=into))
            return last_junk[0]

        def table_chores(c0, c1):
            n = c1 - c0
            sl = slice(c0, c1)
            tok = {}
            dl, pen, hi = wrk[:, 0, 0:n, :], wrk[:, 1, 0:n, :], wrk[:, 2, 0:n, :].bitcast(I32)
            srcs = win[:, 0:n, :, 0]

            def samples_of(c):
                def do():
                    act.need(t_c)
                    tok["s1"] = count_below(smp_i[:, :], c, R, s1[:, c:c + 1])
                return do

            def rows_of():
                dve.need(tok["s1"])
                seq(dve, nc.vector.tensor_scalar(row[:, sl], s1[:, sl], 0.5, R / 2.0 - 1.0, ALU.mult, ALU.add))
                t = dve.mark(nc.vector.tensor_scalar(row_i[:, sl], row[:, sl], 0.0, None, ALU.max))
                pool.need(t)
                for c in range(c0, c1):
                    k = c - c0
                    pool.need(*row_free[k])
                    tok["row", c] = q_row[k].mark(nc.gpsimd.indirect_dma_start(
                        out=rows_i[:, k, :], out_offset=None, in_=dst_rows,
                        in_offset=bass.IndirectOffsetOnAxis(ap=row_i[:, c:c + 1], axis=0)))

            def in_row(c):
                def do():
                    act.need(tok["row", c])
                    tok["s2"] = count_below(rows_i[:, c - c0, :], c, 256, s2[:, c:c + 1])
                    row_free[c - c0] = [tok["s2"]]
                return do

            def windows():
                dve.need(tok["s2"])
                seq(dve, nc.vector.tensor_scalar(off[:, sl], s2[:, sl], 0.5, 128.0, ALU.mult, ALU.add))
                t = dve.mark(nc.vector.scalar_tensor_tensor(first_i[:, sl], row_i[:, sl], 256.0, off[:, sl],
                                                            ALU.mult, ALU.add))
                pool.need(t)
                for c in range(c0, c1):
                    w = c - c0
                    pool.need(*win_free[w])
                    tok["win", c] = q_win[w].mark(nc.gpsimd.indirect_dma_start(
                        out=win[:, w, :, :].rearrange("p n two -> p (n two)"), out_offset=None, in_=flat_pairs,
                        in_offset=bass.IndirectOffsetOnAxis(ap=first_i[:, c:c + 1], axis=0)))

            def from_first(c):
                def do():
                    w, k = c - c0, c - c0
                    dve.need(tok["win", c], *wrk_free)
                    t = dve.mark(nc.vector.tensor_scalar(wrk[:, 0, k, :], win[:, w, :, 1], thr[:, c:c + 1], None,
                                                         ALU.subtract))
                    tok["dl", c] = t
                return do

            def degrees(c):
                def do():
                    act.need(tok["dl", c], t_set)
                    for i in range(GD + 1):
                        act.need(last_junk[0])
                        last_junk[0] = act.mark(nc.scalar.activation(
                            junk[:, 0:P], wrk[:, 0, c - c0, :], ACT.Sign, bias=cut[:, i:i + 1], scale=-1.0,
                            accum_out=sgn[:, c, i:i + 1]))
                    tok["sgn"] = wrk_free[1] = last_junk[0]
                return do

            def positions():
                q = pool if c0 > 1 else dve
                q.need(tok["dl", c1 - 1], tok["hi"])
                seq(q, q.eng.tensor_scalar(pen, dl, GD - 0.5, 1000.0, ALU.is_ge, ALU.mult))
                tok["pen"] = seq(q, q.eng.tensor_tensor(pen, pen, dl, ALU.add))

            def in_tile():
                dve.need(tok["dl", c1 - 1])
                tok["hi"] = seq(dve, nc.vector.tensor_scalar(hi, srcs, 7, None, ALU.logical_shift_right))

            def ready():
                dve.need(tok["pen"])
                seq(dve, nc.vector.scalar_tensor_tensor(pen, hi, float(GD), pen, ALU.mult, ALU.add))
                t = dve.mark(nc.vector.scalar_tensor_tensor(wrk[:, 2, 0:n, :], hi, -128.0, srcs, ALU.mult, ALU.add))
                tok["v"] = t
                for c in range(c0, c1):
                    win_free[c - c0] = [t]

            def turn(c):
                def do():
                    k, w = c - c0, c % NTAB
                    b = 4
                    pe.need(tok["v"], *free[b])
                    for i, j in ((0, 1), (1, 2)):
                        t = pe.mark(nc.tensor.transpose(bank[b][:, P * i:P * i + P], wrk[:, j, k, :], ident))
                    act.need(t, *tab_free[w])
                    t_tab[c] = act.mark(nc.scalar.copy(tab[:, w, :, :].rearrange("p v g -> p (v g)"),
                                                       bank[b][:, 0:2 * P]))
                    free[b] = [t_tab[c]]
                    wrk_free[0] = t
                return do

            def counts():
                dve.need(tok["sgn"])
                seq(dve, nc.vector.tensor_tensor(cntg[:, sl, :], sgn[:, sl, 1:GD + 1], sgn[:, sl, 0:GD], ALU.subtract))
                t = dve.mark(nc.vector.tensor_reduce(tot[:, c0:c0 + 1], cntg[:, sl, :], AX.XY, ALU.add))
                dve.need(t)
                seq(dve, nc.vector.tensor_scalar(cntg[:, sl, :], cntg[:, sl, :], 0.5, 1.0, ALU.mult, ALU.max))
                t = dve.mark(nc.vector.reciprocal(cntg[:, sl, :], cntg[:, sl, :]))
                sp.need(t)
                t = q_rc.mark(sp.eng.dma_start(
                    rc_dram[BD * c0:BD * c1].rearrange("(c p k) -> p c k", c=n, k=GD), cntg[0:GPB, sl, :]))
                sp.need(t)
                for c in range(c0, c1):
                    t_rc[c] = t

            def rest_():
                pass

            pause = [rest_] * 3 if c0 > 1 else [rest_]
            return {"tok": tok,
                    "samples": [samples_of(c) for c in range(c0, c1)],
                    "rows": [rows_of],
                    "windows": [in_row(c) for c in range(c0, c1)] + pause + [windows],
                    "tables": [from_first(c) for c in range(c0, c1)] + [in_tile, positions] + pause + [ready, rest_]
                    + [turn(c) for c in range(c0, c1)],
                    "counts": [f for c in range(c0, c1) for f in (rest_, degrees(c))][1:] + pause + [counts],
                    "pause": pause, "wait": [rest_] * 5}

        full = NA - 1
        groups = [(a0, min(4, full - a0), P) for a0 in range(0, full, 4)] + [(full, 1, LAST)]
        t_hi = {}
        t_lo = {}
        t_relu = {}

        def ln_stats(k, t_x):
            dve.need(t_x, t_set)
            for a in range(cuts[k], cuts[k + 1]):
                r = P if a < full else LAST
                dve.mark(nc.vector.bn_stats(mvx[0:r, a, :], X[0:r, a, :]))

        def ln_scales():
            dve.need(dve.last())
            col = lambda i: rsx[:, i, :]
            me, mo = mvx[:, :, 1], mvx[:, :, 4]
            dve.mark(nc.vector.tensor_tensor(col(0), me, mo, ALU.add))
            seq(dve, nc.vector.tensor_tensor(col(1), me, mo, ALU.subtract))
            dve.mark(nc.vector.tensor_tensor(col(2), mvx[:, :, 2], mvx[:, :, 5], ALU.add))
            seq(dve, nc.vector.tensor_tensor(col(1), col(1), col(1), ALU.mult))
            seq(dve, nc.vector.tensor_scalar(col(2), col(2), 1.0 / P, None, ALU.mult))
            t = seq(dve, nc.vector.scalar_tensor_tensor(col(2), col(1), 0.25, col(2), ALU.mult, ALU.add))
            act.need(t, t_set)
            t = act.mark(nc.scalar.activation(col(1), col(2), ACT.Sqrt, bias=epsc[:, 0:1]))
            dve.need(t)
            seq(dve, nc.vector.reciprocal(col(2), col(1)))
            seq(dve, nc.vector.tensor_scalar(col(2), col(2), S0, None, ALU.mult))
            return seq(dve, nc.vector.scalar_tensor_tensor(col(3), col(0), -0.5, col(2), ALU.mult, ALU.mult))

        def ln_relu(g, t_scales):
            a0, n, r = groups[g]
            if g % 3 == 2:
                pool.need(t_scales)
                for a in range(a0, a0 + n):
                    t = pool.mark(nc.gpsimd.tensor_scalar(X[0:r, a, :], X[0:r, a, :], rsx[0:r, 2, a:a + 1],
                                                          rsx[0:r, 3, a:a + 1], ALU.mult, ALU.add))
                pool.need(t)
                t_relu[g] = pool.mark(nc.gpsimd.tensor_scalar(X[0:r, a0:a0 + n, :], X[0:r, a0:a0 + n, :], 0.0, None,
                                                              ALU.max))
                return
            act.need(t_scales)
            for a in range(a0, a0 + n):
                t_relu[g] = act.mark(nc.scalar.activation(X[0:r, a, :], X[0:r, a, :], ACT.Relu,
                                                          bias=rsx[0:r, 3, a:a + 1], scale=rsx[0:r, 2, a:a + 1]))

        def ln_parts(g):
            a0, n, r = groups[g]
            dve.need(t_relu[g])
            t_hi[g] = dve.mark(nc.vector.tensor_copy(small[0:r, a0:a0 + n, 0, :], X[0:r, a0:a0 + n, :]))
            pool.need(t_hi[g])
            t_lo[g] = pool.mark(nc.gpsimd.tensor_tensor(small[0:r, a0:a0 + n, 1, :], X[0:r, a0:a0 + n, :],
                                                        small[0:r, a0:a0 + n, 0, :], ALU.subtract))

        def ln_turn(g, b):
            a0, n, r = groups[g]
            pe.need(t_relu[g], *free[b])
            for a in range(a0, a0 + n):
                t = pe.mark(nc.tensor.transpose(bank[b][:, P * (a - a0):P * (a - a0) + r], X[0:r, a, :],
                                                ident[0:r, 0:r]))
            act.need(t)
            w = (n - 1) * P + r
            t = act.mark(nc.scalar.copy(Z[:, 0, P * a0:P * a0 + w], bank[b][:, 0:w]))
            free[b] = [t]
            return t

        def load_rc(c):
            s = c % 2
            sp.need(t_rc[c], *rcb_free[s])
            return q_rcb[s].mark(sp.eng.dma_start(
                rcb[:, s, :], rc_dram[BD * c:BD * c + BD].rearrange("(o n) -> o n", o=1).to_broadcast((P, BD))))

        def load_block(c):
            s = c % 3
            sp.need(t_blocks[c], *colfree[s])
            return q_blk[s].mark(sp.eng.dma_start(ring[:, s, :], C_dram[c, :, :]))

        def agg_mm(c, view, m, a, part, b):
            r = P if a < NA - 1 else LAST
            first, last = (a, part) == (0, 0), (a, part) == (NA - 1, 1)
            mm = nc.tensor.matmul(bank[b][:, 0:BD], view[0:r, a, part, m * P:m * P + P], blk[c % 3][0:r, a, :],
                                  start=first, stop=last)
            return pe.mark(mm) if last else None

        def mean_of(c, nm, banks, t_agg, t_rcb, inv):
            s = c % 2
            dve.need(t_agg, t_rcb, *agm_free[s])
            for m in range(nm):
                sc = inv if isinstance(inv, float) else inv[:, m:m + 1]
                t = dve.mark(nc.vector.scalar_tensor_tensor(agm[:, s, m, :], bank[banks[m]][:, 0:BD], sc,
                                                            rcb[:, s, :], ALU.mult, ALU.mult))
                free[banks[m]] = [t]
            rcb_free[s] = [t]
            return t

        def linear(c, layer, nk, t_mean, *t_h, banks=lin_banks):
            for do in linear_parts(c, layer, nk, t_mean, banks[c % 2], *t_h):
                t = do()
            return t

        def linear_parts(c, layer, nk, t_mean, b, *t_h):
            tok = {}
            zc = [Z[:, m, BD * c:BD * c + BD] for m in range(2)]

            def products():
                s = c % 2
                pe.need(t_mean, *t_h, *free[b])
                for m in range(2):
                    n = 0
                    for w, src in ((wr, Z[:, :, BD * c:BD * c + BD]), (wl, agm[:, s, :, :])):
                        for k in range(nk):
                            t = pe.mark(nc.tensor.matmul(bank[b][:, BD * m:BD * m + BD],
                                                         w[layer][:, k, m * P:m * P + P], src[:, k, :],
                                                         start=(n == 0), stop=(n == 2 * nk - 1)))
                            n += 1
                agm_free[s] = [t]
                tok["pe"] = t

            def biased():
                act.need(tok["pe"])
                for m in range(2):
                    t = act.mark(nc.scalar.activation(zc[m], bank[b][:, BD * m:BD * m + BD],
                                                      ACT.Identity, bias=bias[layer][:, m:m + 1]))
                free[b] = [t]
                tok["z"] = t

            def stats():
                dve.need(tok["z"])
                for m in range(2):
                    t = dve.mark(nc.vector.bn_stats(st[:, m, c, :], zc[m]))
                return t

            return [products, biased, stats]

        def last_linear(c, layer, nk, banks, t_agg, t_rcb, inv, *t_h):
            zb = (7, 0)
            s = c % 2
            pe.need(*t_h, *free[zb[0]], *free[zb[1]])
            for m in range(2):
                for k in range(nk):
                    pe.mark(nc.tensor.matmul(bank[zb[m]][:, 0:BD], wr[layer][:, k, m * P:m * P + P],
                                             Z[:, k, BD * c:BD * c + BD], start=(k == 0), stop=False))
            pe.need(mean_of(c, nk, banks, t_agg, t_rcb, inv))
            t_m = []
            for m in range(2):
                for k in range(nk):
                    t = pe.mark(nc.tensor.matmul(bank[zb[m]][:, 0:BD], wl[layer][:, k, m * P:m * P + P],
                                                 agm[:, s, k, :], start=False, stop=(k == nk - 1)))
                t_m.append(t)
            agm_free[s] = [t]
            for m in range(2):
                act.need(t_m[m])
                t = act.mark(nc.scalar.activation(Z[:, m, BD * c:BD * c + BD], bank[zb[m]][:, 0:BD],
                                                  ACT.Identity, bias=bias[layer][:, m:m + 1]))
                free[zb[m]] = [t]
                dve.need(t)
                t = dve.mark(nc.vector.bn_stats(st[:, m, c, :], Z[:, m, BD * c:BD * c + BD]))
            return t

        batches = [(0, 1)]
        while batches[-1][1] < NB:
            c0 = batches[-1][1]
            c1 = min(NB, c0 + NBT)
            batches.append((c0, c1))
        first = table_chores(*batches[0])
        second = table_chores(*batches[1])
        for chore in first["samples"] + first["rows"] + second["samples"]:
            chore()
        sp.need(first["tok"]["row", 0])
        t_x.append(load_x(2))
        ln_stats(0, t_x[0])
        for chore in first["windows"] + second["rows"]:
            chore()
        ln_stats(1, t_x[1])
        sp.need(first["tok"]["win", 0])
        t_x.append(load_x(3))
        for layer in range(3):
            for w, src in ((wl[layer], WlT[layer]), (wr[layer], WrT[layer])):
                q_w.mark(sp.eng.dma_start(w[:, :, :], src.rearrange("(k p) m -> p k m", p=P)))
        t_w = q_w.mark(sp.eng.dma_start(vec[:, :], vecs))
        for chore in first["tables"] + first["counts"][:-1]:
            chore()
        ln_stats(2, t_x[2])
        for chore in second["windows"]:
            chore()
        ln_stats(3, t_x[3])
        t_scales = ln_scales()
        first["counts"][-1]()
        dve.need(t_w)
        t_wr0 = dve.mark(nc.vector.tensor_scalar(wr[0][:, :, :], wr[0][:, :, :], 1.0 / S0, None, ALU.mult))
        def norm_constants():
            for layer in range(2):
                g, be = gamma[layer], beta[layer]
                w = lambda i: bnw[:, layer, i, :]
                seq(dve, nc.vector.scalar_tensor_tensor(w(3), g, -1.0, g, ALU.mult, ALU.max))
                seq(dve, nc.vector.scalar_tensor_tensor(w(4), be, -1.0, be, ALU.mult, ALU.max))
                seq(dve, nc.vector.scalar_tensor_tensor(w(3), w(3), 1.01 * float(N) ** 0.5, w(4), ALU.mult, ALU.add))
                seq(dve, nc.vector.tensor_scalar(w(3), w(3), 1e-30, None, ALU.max))
                seq(dve, nc.vector.tensor_scalar(w(4).bitcast(I32), w(3).bitcast(I32), 0x7F800000, None,
                                                 ALU.bitwise_and))
                seq(dve, nc.vector.tensor_scalar(w(5).bitcast(I32), w(4).bitcast(I32), -1.0, float(268 << 23),
                                                 ALU.mult, ALU.add))
                seq(dve, nc.vector.tensor_tensor(w(0), g, w(5), ALU.mult))
                seq(dve, nc.vector.tensor_tensor(w(1), be, w(5), ALU.mult))
                seq(dve, nc.vector.tensor_scalar(w(2), w(4), 2.0 ** -14, None, ALU.mult))
                for k in range(2):
                    seq(dve, nc.vector.tensor_scalar(wr[layer + 1][:, k, :], wr[layer + 1][:, k, :],
                                                     w(2)[:, k:k + 1], None, ALU.mult))
            for k in range(2):
                seq(dve, nc.vector.tensor_scalar(wl[2][:, k, :], wl[2][:, k, :], bnw[:, 1, 2, k:k + 1], None, ALU.mult))
            for k in range(2):
                seq(dve, nc.vector.scalar_tensor_tensor(spr[:, k, :], wl[2][:, k, :], -1.0, wl[2][:, k, :],
                                                        ALU.mult, ALU.max))
            yield
            pe.need(dve.last(), *free[0])
            for k in range(2):
                t = pe.mark(nc.tensor.matmul(bank[0][:, 0:P], ones[:, :], spr[:, k, :], start=(k == 0), stop=(k == 1)))
            dve.need(t)
            seq(dve, nc.vector.tensor_scalar(spr[:, 2, :], bank[0][:, 0:P], 2.0 ** 15 * 1.01, 1e-30, ALU.mult, ALU.max))
            free[0] = [dve.last()]
            seq(dve, nc.vector.tensor_scalar(spi[:, 0, :], spr[:, 2, :].bitcast(I32), 0x7F800000, None,
                                             ALU.bitwise_and))
            seq(dve, nc.vector.tensor_scalar(spi[:, 1, :], spi[:, 0, :], -1.0, float(268 << 23), ALU.mult, ALU.add))
            for k in range(2):
                seq(dve, nc.vector.tensor_tensor(wl[2][:, k, :], wl[2][:, k, :], spi[:, 1, :].bitcast(F32), ALU.mult))
            t_w2 = seq(dve, nc.vector.tensor_scalar(spr[:, 0, :], spi[:, 0, :].bitcast(F32), 2.0 ** -14, None,
                                                    ALU.mult))
            yield
            pe.need(t_w2, *free[0])
            t = pe.mark(nc.tensor.transpose(bank[0][:, 0:P], spr[:, 0, :], ident))
            dve.need(t)
            t_isp = seq(dve, nc.vector.tensor_copy(isp[:, :], bank[0][:, 0:1]))
            free[0] = [t_isp]
            yield t_isp

        def edges_found():
            cols = [c0 for c0, _ in batches]
            dve.need(dve.last())
            seq(dve, nc.vector.tensor_copy(tot[:, NB:NB + 1], tot[:, cols[0]:cols[0] + 1]))
            for c0 in cols[1:]:
                seq(dve, nc.vector.tensor_tensor(tot[:, NB:NB + 1], tot[:, NB:NB + 1], tot[:, c0:c0 + 1], ALU.add))
            yield
            pe.need(dve.last(), t_set, *free[0])
            t = pe.mark(nc.tensor.matmul(bank[0][:, 0:1], ones[0:GPB, :], tot[0:GPB, NB:NB + 1], start=True, stop=True))
            dve.need(t)
            t = dve.mark(nc.vector.tensor_scalar(flag[:, :], bank[0][:, 0:1], 2.0 * E, None, ALU.is_equal))
            free[0] = [t]
            yield t

        hot_free = [[] for _ in range(NHOT)]
        build_banks = [0, 1, 5, 6]
        steps = [0]
        pending = []
        pending += second["tables"]
        made = second
        todo = batches[2:]

        def build_step(c, i):
            n = min(GPS, GPB - GPS * i)
            q = (n + 1) // 2
            s = steps[0] % NHOT
            w = c % NTAB
            ps = hot[:, s, 0:GPS * NW].rearrange("p (q x t) -> p q x t", x=NW, t=2)
            bs = hot[:, s, GPS * NW:HOT].rearrange("p (q x t) -> p q x t", x=P, t=2)
            dve.need(t_tab[c], t_c, *hot_free[s])
            for v, o, x_ in ((1, bs, P), (0, ps, NW)):
                pos = tab[:, w, v, GPS * i:GPS * i + 2 * q].rearrange("p (q t) -> p q t", t=2)
                t = dve.mark(nc.vector.tensor_tensor(
                    o[:, 0:q, :, :], iota2[:, 0:x_, :].unsqueeze(1).to_broadcast((P, q, x_, 2)),
                    pos.unsqueeze(2).to_broadcast((P, q, x_, 2)), ALU.is_equal))
            tab_free[w] = [t]
            pe.need(t)
            for g0 in range(0, n, GPK):
                b = build_banks[(2 * steps[0] + g0 // GPK) % 4]
                pe.need(*free[b])
                for g in range(g0, g0 + GPK):
                    t = pe.mark(nc.tensor.matmul(bank[b][:, NW * (g - g0):NW * (g - g0) + NW],
                                                 bs[:, g // 2, :, g % 2], ps[:, g // 2, :, g % 2],
                                                 start=True, stop=True))
                hot_free[s] = [t]
                act.need(t, *(colfree[c % 3] if i == 0 else []))
                d0 = GD * (GPS * i + g0)
                t = act.mark(nc.scalar.copy(
                    blk[c % 3][:, :, d0:d0 + GD * GPK].rearrange("p a (g d) -> p a g d", d=GD),
                    bank[b][:, 0:GPK * NW].rearrange("p (g a d) -> p a g d", g=GPK, d=GD)))
                free[b] = [t]
            steps[0] += 1
            return t

        ln_relu(0, t_scales)
        for c in range(NB + 1):
            if c < NB:
                if c in [b0 for b0, _ in batches[1:]]:
                    pending += made["counts"]
                while todo and todo[0][0] <= c + NBT and c:
                    made = table_chores(*todo.pop(0))
                    pending += [chore for k in ("samples", "pause", "rows", "wait", "windows", "wait", "tables")
                                for chore in made[k]]
                left = max(1, (min([b0 for b0, _ in batches if b0 > c] + [10 ** 6]) - c)) * NST
            if c == NB:
                constants, found = norm_constants(), edges_found()
            if c >= 1:
                work = [(a, part) for a in range(NA) for part in range(2)]
                b = (3, 2)[c % 2]
                t_rcb = load_rc(c - 1)
                pe.need(t_built, *free[b])
                done = 0
            for i in range(NST):
                if c < NB:
                    t = build_step(c, i)
                    for _ in range(-(-len(pending) // (left - i))):
                        pending.pop(0)()
                if c == 0:
                    for _ in range(-(-len(groups) // NST)):
                        if len(t_relu) < len(groups):
                            ln_relu(len(t_relu), t_scales)
                        if len(t_lo) + 2 < len(t_relu):
                            ln_parts(len(t_lo))
                if c >= 1:
                    upto = len(work) * (i + 1) // NST
                    for a, part in work[done:upto]:
                        if c == 1:
                            pe.need(t_lo[min(g for g, (a0, n, _) in enumerate(groups) if a < a0 + n)])
                        t_agg = agg_mm(c - 1, small, 0, a, part, b)
                    done = upto
                if c >= 2:
                    if i == 2:
                        act.need(t_hi[len(groups) - 1], t_lo[len(groups) - 1])
                        t_mean = mean_of(c - 2, 1, sums[0], sums[1], sums[2], 1.0 / S0)
                        parts_left = linear_parts(c - 2, 0, 1, t_mean, 7, t_h0, t_wr0)
                    elif i in (4, 6, 11):
                        parts_left.pop(0)()
                if c == NB:
                    if i == 2:
                        next(found)
                        next(constants)
                    elif i == 7:
                        next(constants)
                    elif i == 9:
                        t_flag = next(found)
                    elif i == 10:
                        t_const = next(constants)
                if c >= 1 and i == 10 and c <= len(groups):
                    t_h0 = ln_turn(c - 1, 7)
            if c == 0:
                while len(t_lo) < len(groups):
                    ln_parts(len(t_lo))
            if c < NB:
                t_built = t_loaded[c] = t
                sp.need(t)
                t_blocks[c] = q_st[c % 3].mark(sp.eng.dma_start(C_dram[c, :, :], ring[:, c % 3, :]))
            if c >= 1:
                colfree[(c - 1) % 3] = [t_agg, t_blocks[c - 1]]
                sums = ([b], t_agg, t_rcb)
        t_l0 = last_linear(NB - 1, 0, 1, *sums, 1.0 / S0, t_h0, t_wr0)

        for s in streams:
            s.need(t_flag)
        taken = nc.values_load(flag[0:1, 0:1], min_val=0, max_val=1)

        def rest(fast):
            def tab_rows(F):
                return tab_dram[0:N * 2 * F].rearrange("(r f) -> r f", f=2 * F)

            def dump_parts(view, F, *made):
                sp.need(*made)
                for a0, a1, rows in ((0, NA - 1, P), (NA - 1, NA, LAST)):
                    tk = q_tab.mark(sp.eng.dma_start(
                        tab_rows(F)[a0 * P:a0 * P + (a1 - a0) * rows, :].rearrange("(a p) f -> p a f", p=rows),
                        view[0:rows, a0:a1, :, :].rearrange("p a s f -> p a (s f)")))
                pool.need(tk)

            def slow_block(c, F, banks, with_count):
                nm = F // P
                for m in range(nm):
                    pe.need(*free[banks[m]])
                if with_count:
                    pe.need(*free[1])
                outs = [bank[banks[m]][:, 0:BD] for m in range(nm)] + ([bank[1][:, 0:BD]] if with_count else [])
                for o in outs:
                    nc.tensor.matmul(o, ones_h[:, :], zeros_h[:, :], start=True, stop=False, skip_group_check=True)
                G = slow_g[:, 0:2 * F]
                with nc.Fori(0, NT) as i:
                    nc.gpsimd.wait_ge(s_it["pe"], i + 1)
                    nc.gpsimd.tensor_copy(slow_i[:, :], ed[:, bass.ds(i, 1), 0]).then_inc(s_it["idx"], 1)
                    nc.gpsimd.wait_ge(s_it["idx"], i + 1)
                    nc.gpsimd.sem_inc(s_it["go"])
                    nc.gpsimd.indirect_dma_start(
                        out=G, out_offset=None, in_=tab_rows(F),
                        in_offset=bass.IndirectOffsetOnAxis(ap=slow_i[:, 0:1], axis=0)).then_inc(s_g, 16)
                    nc.vector.wait_ge(s_it["pe"], i + 1)
                    nc.vector.tensor_scalar(slow_f[:, 0:1], ed[:, bass.ds(i, 1), 1], float(-BD * c), None,
                                            ALU.add).then_inc(s_it["col"], 1)
                    nc.vector.wait_ge(s_it["col"], i + 1)
                    nc.vector.tensor_scalar(slow_o, iota[:, 0:BD], slow_f[:, 0:1], None,
                                            ALU.is_equal).then_inc(s_it["hot"], 1)
                    nc.tensor.wait_ge(s_it["hot"], i + 1)
                    nc.tensor.wait_ge(s_g, (i + 1) * 16)
                    for part in range(2):
                        for m in range(nm):
                            mm = nc.tensor.matmul(outs[m], G[:, part * F + m * P:part * F + m * P + P], slow_o,
                                                  start=False, stop=False, skip_group_check=True)
                    if with_count:
                        mm = nc.tensor.matmul(outs[-1], ones_h[:, :], slow_o, start=False, stop=False,
                                              skip_group_check=True)
                    mm.then_inc(s_it["pe"], 1)
                for o in outs:
                    t = pe.mark(nc.tensor.matmul(o, ones_h[:, :], zeros_h[:, :], start=False, stop=True,
                                                 skip_group_check=True))
                dve.need(t)
                t_v = dve.mark(nc.vector.memset(slow_f[:, 1:2], 0.0))
                pool.need(t, t_v)
                nc.gpsimd.inc_swdge_sem([s_g], [NT * 16], mode="sub")
                for k in ("idx", "hot", "pe", "col", "go"):
                    nc.gpsimd.sem_clear(s_it[k])
                t_z = pool.mark(nc.gpsimd.memset(slow_i[:, :], 0))
                dve.need(t_z)
                pe.need(t_z)
                nc.tensor.sem_inc(s_it["pe"], 1)
                return t

            if fast:
                t_end = t_l0
            else:
                for s in streams:
                    s.need(*[o.last() for o in streams if o.n], *[(o.sem, o.n) for o in slots if o.n])
                t_ed = q_tab.mark(sp.eng.dma_start(
                    ed, flat_pairs[0:NT * P, :].rearrange("(p t) two -> p t two", p=P)))
                for s in streams:
                    s.need(t_ed)
                nc.tensor.sem_inc(s_it["pe"], 1)
                for k in range(4):
                    ln_stats(k, load_x(k))
                t_scales = ln_scales()
                for g in range(len(groups)):
                    ln_relu(g, t_scales)
                    ln_parts(g)
                    h0 = ln_turn(g, (3, 7)[g % 2])
                lo0 = pool.last()
                dump_parts(small, 128, h0, lo0)
                for c in range(NB):
                    t = slow_block(c, 128, [3], True)
                    s = c % 2
                    dve.need(t, (q_rc.sem, q_rc.n), *rcb_free[s])
                    seq(dve, nc.vector.tensor_scalar(rcb[:, s, :], bank[1][:, 0:BD], 1.0, None, ALU.max))
                    free[1] = [dve.last()]
                    t_r = seq(dve, nc.vector.reciprocal(rcb[:, s, :], rcb[:, s, :]))
                    sp.need(t_r)
                    t_rc[c] = q_rc.mark(sp.eng.dma_start(
                        rc_dram[BD * c:BD * c + BD].rearrange("(o n) -> o n", o=1), rcb[0:1, s, :]))
                    t_end = linear(c, 0, 1, mean_of(c, 1, [3], t, None, 1.0 / S0), h0, lo0)
                for s in streams:
                    s.need(t_rc[NB - 1])

            def batch_norm(layer):
                w = lambda i: bnw[:, layer, i, :]
                dve.need(dve.last())
                for m in range(2):
                    dve.mark(nc.vector.bn_aggr(mv[:, m, :], st[:, m, 0:NB, :]))
                act.need(dve.last(), t_const)
                t = act.mark(nc.scalar.activation(bnt[:, 0, :], mv[:, :, 1], ACT.Sqrt, bias=epsc[:, 0:1]))
                dve.need(t, dve.last())
                seq(dve, nc.vector.reciprocal(bnt[:, 1, :], bnt[:, 0, :]))
                seq(dve, nc.vector.tensor_tensor(w(4), bnt[:, 1, :], w(0), ALU.mult))
                seq(dve, nc.vector.tensor_tensor(bnt[:, 2, :], mv[:, :, 0], w(4), ALU.mult))
                t = seq(dve, nc.vector.tensor_tensor(w(5), w(1), bnt[:, 2, :], ALU.subtract))
                return t, w(4), w(5), w(2)

            def relu_cols(t_bn, sc, sh, c0, w):
                act.need(t_bn)
                for k in range(2):
                    t = act.mark(nc.scalar.activation(Z[:, k, c0:c0 + w], Z[:, k, c0:c0 + w], ACT.Relu,
                                                      bias=sh[:, k:k + 1], scale=sc[:, k:k + 1]))
                return t

            def split(b, view, a0, n, F, t_pe):
                full = n if a0 + n < NA else n - 1
                pieces = ([(P, 0, full)] if full else []) + ([(LAST, full, n)] if full < n else [])
                act.need(t_pe)
                src = lambda r, i, k: bank[b][0:r, i * F:k * F].rearrange("p (a f) -> p a f", a=k - i)
                for r, i, k in pieces:
                    t = act.mark(nc.scalar.copy(view[0:r, a0 + i:a0 + k, 0, :], src(r, i, k)))
                dve.need(t)
                for r, i, k in pieces:
                    t = dve.mark(nc.vector.tensor_tensor(view[0:r, a0 + i:a0 + k, 1, :], src(r, i, k),
                                                         view[0:r, a0 + i:a0 + k, 0, :], ALU.subtract))
                free[b] = [t]
                return t

            t_bn, sc, sh, inv1 = batch_norm(0)

            def prep_turn(t, t_r, b):
                a0 = 2 * t
                pe.need(t_r, *free[b])
                for a in range(a0, min(a0 + 2, NA)):
                    r = P if a < NA - 1 else LAST
                    for k in range(2):
                        o = 256 * (a - a0) + 128 * k
                        tk = pe.mark(nc.tensor.transpose(bank[b][0:r, o:o + 128],
                                                         Z[:, k, 128 * a:128 * a + r], ident))
                return tk

            def prepare(n, width, turn, view, F, use):
                def relu(t):
                    a1 = min(NA, width * (t + 1))
                    return relu_cols(t_bn, sc, sh, 128 * width * t, min(N, 128 * a1) - 128 * width * t)

                def turned(t):
                    b = [0, 1, 2][t % 3]
                    tk = turn(t, t_r.pop(t), b)
                    return split(b, view, width * t, min(width, NA - width * t), F, tk)

                t_r = {t: relu(t) for t in range(min(2, n))}
                t_s = turned(0)
                for t in range(n):
                    if t + 2 < n:
                        t_r[t + 2] = relu(t + 2)
                    t_next = turned(t + 1) if t + 1 < n else None
                    use(t, t_s)
                    t_s = t_next

            npair = -(-NA // 2)
            order = list(range(NB))[::-1]
            if fast:
                bb = {c: [(3, 4), (5, 6)][j % 2] for j, c in enumerate(order)}
                pend = []

                def agg1(c, tiles):
                    for a in tiles:
                        for part in range(2):
                            for m in range(2):
                                t = agg_mm(c, wide, m, a, part, bb[c][m])
                    return t

                def done1(j, t_agg, t_rcb):
                    c = order[j]
                    colfree[c % 3] = [t_agg]
                    if j + 3 < NB:
                        t_loaded[order[j + 3]] = load_block(order[j + 3])
                    pend.append((c, 1, 2, mean_of(c, 2, bb[c], t_agg, t_rcb, inv1)))

                heads = order[:2]
                t_rcb = {c: load_rc(c) for c in heads}
                t_aggs = {}
                for c in heads:
                    pe.need(t_loaded[c], *free[bb[c][0]], *free[bb[c][1]])

                def both(t, t_s):
                    pe.need(t_s)
                    for c in heads:
                        t_aggs[c] = agg1(c, range(2 * t, min(2 * t + 2, NA)))

                prepare(npair, 2, prep_turn, wide, 256, both)
                for j, c in enumerate(heads):
                    done1(j, t_aggs[c], t_rcb[c])
                for j in range(len(heads), NB):
                    c = order[j]
                    t_rcb = load_rc(c)
                    pe.need(t_loaded[c], *free[bb[c][0]], *free[bb[c][1]])
                    for a in range(NA):
                        t_agg = agg1(c, [a])
                        if a in (NA // 8, NA // 4) and pend:
                            linear(*pend.pop(0))
                    if j < NB - 1:
                        done1(j, t_agg, t_rcb)
                while pend:
                    linear(*pend.pop(0))
                t_last = last_linear(c, 1, 2, bb[c], t_agg, t_rcb, inv1)
                colfree[c % 3] = [t_agg]
            else:
                prepare(npair, 2, prep_turn, wide, 256, lambda t, t_s: None)
                dump_parts(wide, 256, act.last(), dve.last())
                for c in range(NB):
                    t_rcb = load_rc(c)
                    t = slow_block(c, 256, [3, 4], False)
                    t_last = linear(c, 1, 2, mean_of(c, 2, [3, 4], t, t_rcb, inv1))

            t_bn, sc, sh, _ = batch_norm(1)
            nquad = -(-NA // 4)

            def prep_product(t, t_r, b):
                a0 = 4 * t
                pe.need(t_r, t_const, *free[b])
                for a in range(a0, min(a0 + 4, NA)):
                    r = P if a < NA - 1 else LAST
                    for k in range(2):
                        tk = pe.mark(nc.tensor.matmul(bank[b][0:r, 128 * (a - a0):128 * (a - a0) + 128],
                                                      Z[:, k, 128 * a:128 * a + r], wl[2][:, k, :],
                                                      start=(k == 0), stop=(k == 1)))
                return tk

            sp.need(pe.last(), act.last(), dve.last(), t_last)
            for a0, a1, rows in ((0, NA - 1, P), (NA - 1, NA, LAST)):
                t_xr = q_xr.mark(sp.eng.dma_start(
                    xres[0:rows, a0:a1, :],
                    x[a0 * P:a0 * P + (a1 - a0) * rows, :].rearrange("(a p) f -> p a f", p=rows)))

            def linear2(c, t_mean):
                s = c % 2
                b = 7
                pe.need(*free[b])
                for k in range(2):
                    t = pe.mark(nc.tensor.matmul(bank[b][:, 0:BD], wr[2][:, k, :], Z[:, k, BD * c:BD * c + BD],
                                                 start=(k == 0), stop=(k == 1)))
                dve.need(t, t_mean)
                t = dve.mark(nc.vector.scalar_tensor_tensor(Z[:, 0, BD * c:BD * c + BD], bank[b][:, 0:BD],
                                                            bias[2][:, 0:1], agm[:, s, 0, :], ALU.add, ALU.add))
                free[b] = [t]
                agm_free[s] = [t]
                return t

            fin = [0, 0]
            o_tok = [None] * 4

            def final(t_z, upto):
                while fin[0] < NA:
                    a0 = fin[0]
                    n = min(2, NA - a0)
                    if a0 + n == NA and n == 2 and LAST < P:
                        n = 1
                    w = min(N, 128 * (a0 + n)) - 128 * a0
                    if 128 * a0 + w > upto:
                        return
                    r = P if a0 + n < NA else LAST
                    u = fin[1]
                    fin[0] += n
                    fin[1] += 1
                    b = [0, 1, 2][u % 3]
                    s = u % 4
                    pe.need(t_z, *free[b])
                    for i in range(n):
                        t = pe.mark(nc.tensor.transpose(bank[b][0:r, 128 * i:128 * i + 128],
                                                        Z[:, 0, 128 * (a0 + i):128 * (a0 + i) + r], ident))
                    v = bank[b][0:r, 0:128 * n].rearrange("p (a f) -> p a f", a=n)
                    dve.need(t, o_tok[s])
                    seq(dve, nc.vector.tensor_reduce(sm[0:r, 0, a0:a0 + n], v, AX.X, ALU.max))
                    t = seq(dve, nc.vector.tensor_tensor(dd[0:r, s, 0:n, :], v,
                                                         sm[0:r, 0, a0:a0 + n].unsqueeze(2).to_broadcast((r, n, P)),
                                                         ALU.subtract))
                    free[b] = [t]
                    act.need(t)
                    for i in range(n):
                        t = act.mark(nc.scalar.activation(ex[0:r, i, :], dd[0:r, s, i, :], ACT.Exp,
                                                          accum_out=sm[0:r, 1, a0 + i:a0 + i + 1]))
                    act.need(t)
                    t = act.mark(nc.scalar.activation(sm[0:r, 2, a0:a0 + n], sm[0:r, 1, a0:a0 + n], ACT.Ln))
                    dve.need(t, t_xr)
                    for i in range(n):
                        t = dve.mark(nc.vector.scalar_tensor_tensor(
                            dd[0:r, s, i, :], dd[0:r, s, i, :], sm[0:r, 2, a0 + i:a0 + i + 1], xres[0:r, a0 + i, :],
                            ALU.subtract, ALU.add))
                    sp.need(t)
                    o_tok[s] = q_o[s].mark(sp.eng.dma_start(
                        out[128 * a0:128 * a0 + (n - 1) * 128 + r, :].rearrange("(a p) f -> p a f", p=r),
                        dd[0:r, s, 0:n, :]))

            if fast:
                bank2 = lambda c: [3, 4][c % 2]
                heads = list(range(min(2, NB)))
                t_aggs = {}
                t_rcb = {c: load_rc(c) for c in heads}
                for c in heads:
                    pe.need(t_loaded[c], *free[bank2(c)])

                def agg2(c, tiles):
                    for a in tiles:
                        for part in range(2):
                            t = agg_mm(c, small, 0, a, part, bank2(c))
                    return t

                def done2(c, t_agg, t_rcb):
                    colfree[c % 3] = [t_agg]
                    if c + 3 < NB:
                        t_loaded[c + 3] = load_block(c + 3)
                    pend.append((c, mean_of(c, 1, [bank2(c)], t_agg, t_rcb, isp)))

                def both2(t, t_s):
                    pe.need(t_s)
                    for c in heads:
                        t_aggs[c] = agg2(c, range(4 * t, min(4 * t + 4, NA)))

                prepare(nquad, 4, prep_product, small, 128, both2)
                act.eng.preload_act_table_set("natural_log_exp_and_others")
                pend = []
                for c in heads:
                    done2(c, t_aggs[c], t_rcb[c])
                for c in range(len(heads), NB):
                    t_rcb = load_rc(c)
                    pe.need(t_loaded[c], *free[bank2(c)])
                    ready = []
                    for a in range(NA):
                        t_agg = agg2(c, [a])
                        if a in (NA // 4, NA // 2) and pend:
                            ready = [(linear2(*pend[0]), BD * (pend[0][0] + 1))]
                            pend.pop(0)
                    done2(c, t_agg, t_rcb)
                    for r in ready:
                        final(*r)
                for p_ in pend:
                    final(linear2(*p_), BD * (p_[0] + 1))
            else:
                prepare(nquad, 4, prep_product, small, 128, lambda t, t_s: None)
                act.eng.preload_act_table_set("natural_log_exp_and_others")
                dump_parts(small, 128, act.last(), dve.last())
                for c in range(NB):
                    t_rcb = load_rc(c)
                    t = slow_block(c, 128, [3], False)
                    t_z = linear2(c, mean_of(c, 1, [3], t, t_rcb, isp))
                    final(t_z, BD * (c + 1))
            for t in o_tok + [(s.sem, s.n) for s in q_st + [q_rc, q_tab]]:
                if t and t[1]:
                    sp.need(t)

        kept = ([s.state() for s in streams], [s.n for s in slots], {k: list(v) for k, v in free.items()},
                [list(v) for v in agm_free], [list(v) for v in rcb_free])
        with nc.If(taken):
            rest(True)
        with nc.Else():
            for s, v in zip(streams, kept[0]):
                s.restore(v)
            for s, v in zip(slots, kept[1]):
                s.n = v
            free.update(kept[2])
            agm_free[:], rcb_free[:] = kept[3], kept[4]
            rest(False)


def kernel(**inputs):
    import numpy as _np
    import concourse.bacc as _bacc
    from concourse import mybir as _mybir
    from concourse.bass_utils import run_bass_kernel_spmd as _run

    x = _np.ascontiguousarray(inputs["x"])
    src = _np.asarray(inputs["src"])
    dst = _np.asarray(inputs["dst"])
    N = x.shape[0]
    E = src.shape[0]
    R = -(-E // 256)
    EP = (R + 1) * 256
    pad = 2 * N + 1000
    NA = -(-N // 128)
    NB = N // BD
    pairs = _np.zeros((EP, 2), src.dtype)
    pairs[:, 1] = pad
    pairs[:E, 0] = src
    pairs[:E, 1] = dst
    dst_rows = _np.ascontiguousarray(pairs[:R * 256, 1].reshape(R, 256))
    const_f = _np.zeros((128, 2 * NB + 128), _np.float32)
    const_f[:, :NB] = BD * _np.arange(NB)[None, :] + GD * _np.arange(128)[:, None]
    const_f[:, NB:2 * NB] = const_f[:, :NB] - 0.5
    const_f[:, 2 * NB:] = _np.eye(128)
    iota = _np.zeros((128, 512), _np.float16)
    iota[:, :256] = _np.arange(256)
    iota[:, 256:] = _np.repeat(_np.arange(128), 2)

    def col(n):
        return _np.asarray(inputs["L0_gnn_" + n]).reshape(-1, 128).T

    vecs = _np.ascontiguousarray(_np.concatenate(
        [col(n) for n in ("bl0", "bl1", "bl2", "gamma0", "gamma1", "beta0", "beta1")], axis=1))
    arrays = {
        "x": x, "pairs": pairs.reshape(R + 1, 256, 2), "dst_rows": dst_rows,
        "samples": _np.ascontiguousarray(dst_rows[:, 0].reshape(1, R)),
        "const_f": const_f, "iota": iota, "vecs": vecs,
    }
    for i in range(3):
        for n in ("Wl", "Wr"):
            arrays[f"{n}T{i}"] = _np.ascontiguousarray(_np.asarray(inputs[f"L0_gnn_{n}{i}"]).T)

    nc = _bacc.Bacc("TRN2", target_bir_lowering=False, num_devices=1)
    named = {f"in_{k}_dram": v for k, v in arrays.items()}
    ap = {k: nc.dram_tensor(f"in_{k}_dram", v.shape, _mybir.dt.from_np(v.dtype), kind="ExternalInput").ap()
          for k, v in arrays.items()}
    out = nc.dram_tensor("out_0_dram", x.shape, _mybir.dt.from_np(x.dtype), kind="ExternalOutput").ap()
    gnn_program(nc, E, ap["x"], ap["pairs"], ap["dst_rows"], ap["samples"], ap["const_f"], ap["iota"],
                [ap[f"WlT{i}"] for i in range(3)], [ap[f"WrT{i}"] for i in range(3)], ap["vecs"], out)
    r = _run(nc, [named], core_ids=[0])
    return r.results[0]["out_0_dram"]
```
